# Optimizing a Trainium2 kernel written in Bass

```python
import numpy as np
import jax
import jax.numpy as jnp

def _softmax(x, axis=-1):
    return jax.nn.softmax(x, axis=axis)

def _gelu(x):
    return jax.nn.gelu(x, approximate=True)

def _silu(x):
    return jax.nn.silu(x)

def _sigmoid(x):
    return jax.nn.sigmoid(x)

def _layernorm(x, axis=-1, eps=1e-05):
    m = jnp.mean(x, axis=axis, keepdims=True)
    v = jnp.var(x, axis=axis, keepdims=True)
    return (x - m) / jnp.sqrt(v + eps)

def _scatter_add(tgt, idx, src, axis=0):
    return tgt.at[idx].add(src)

def _segment_sum(src, seg, n):
    return jax.ops.segment_sum(src, seg, n)
kernel_name = 'mk_adaln_d1_jaxref_r8_e1b811'

def setup_inputs(seed: int=0):
    np.random.seed(seed)
    _w = jnp.asarray

    def _L0_attn_setup():
        import jax, jax.numpy as jnp
        import numpy as np
        MAX_DIST = 8
        GUIDANCE_WEIGHT = 0.4
        EPS_MAG = 1e-06
        EPS_COS = 1e-08
        EPS_WSUM = 1e-08
        key = jax.random.key(seed)
        k1, k2 = jax.random.split(key)
        embeddings = jax.random.normal(k1, (4, 256, 128), dtype=jnp.float32)
        guidance_trajectories = jax.random.normal(k2, (64, 128), dtype=jnp.float32)
        return {'embeddings': embeddings, 'guidance_trajectories': guidance_trajectories}
    _L0_attn_in = _L0_attn_setup()

    def _L0_ffn_setup():
        import jax, jax.numpy as jnp
        import numpy as np
        DIM = 128
        DEPTH = 2
        HEADS = 8
        DIM_HEAD = 64
        WINDOW = 64
        INNER = HEADS * DIM_HEAD
        HID = int(DIM * 4 * 2 / 3)
        B, N = (2, 1024)
        QK_SCALE = 8.0

        def shift_token(t):
            t1, t2 = jnp.split(t, 2, axis=-1)
            t2 = jnp.pad(t2, ((0, 0), (1, 0), (0, 0)))[:, :-1]
            return jnp.concatenate([t1, t2], axis=-1)

        def l2norm(t):
            return t / jnp.clip(jnp.linalg.norm(t, axis=-1, keepdims=True), 1e-12)

        def rotate_half(x):
            x1, x2 = jnp.split(x, 2, axis=-1)
            return jnp.concatenate([-x2, x1], axis=-1)

        def rotary_xpos(q, k):
            n = q.shape[-2]
            half_idx = jnp.arange(0, DIM_HEAD, 2, dtype=jnp.float32)
            inv_freq = 1.0 / 10000.0 ** (half_idx / DIM_HEAD)
            t = jnp.arange(n, dtype=jnp.float32)
            freqs = t[:, None] * inv_freq[None, :]
            freqs = jnp.concatenate([freqs, freqs], axis=-1)
            base = (half_idx + 0.4 * DIM_HEAD) / (1.4 * DIM_HEAD)
            power = (t - n // 2) / float(WINDOW // 2)
            scale = base[None, :] ** power[:, None]
            scale = jnp.concatenate([scale, scale], axis=-1)
            cos, sin = (jnp.cos(freqs), jnp.sin(freqs))
            q = q * cos * scale + rotate_half(q) * sin * scale
            k = k * cos / scale + rotate_half(k) * sin / scale
            return (q, k)

        def local_attention(q, k, v):
            b, h, n, d = q.shape
            w = n // WINDOW
            bq = q.reshape(b, h, w, WINDOW, d) * QK_SCALE
            bk = k.reshape(b, h, w, WINDOW, d)
            bv = v.reshape(b, h, w, WINDOW, d)

            def look_around(t):
                p = jnp.pad(t, ((0, 0), (0, 0), (1, 0), (0, 0), (0, 0)))
                return jnp.concatenate([p[:, :, :w], p[:, :, 1:]], axis=3)
            bk, bv = (look_around(bk), look_around(bv))
            bt = jnp.arange(n).reshape(w, WINDOW)
            btp = jnp.pad(bt, ((1, 0), (0, 0)), constant_values=-1)
            btk = jnp.concatenate([btp[:w], btp[1:]], axis=1)
            sim = jnp.einsum('bhwid,bhwjd->bhwij', bq, bk)
            i = bt[:, :, None]
            j = btk[:, None, :]
            mask = (i < j) | (i > j + WINDOW) | (j == -1)
            sim = jnp.where(mask, -jnp.finfo(sim.dtype).max, sim)
            attn = jax.nn.softmax(sim, axis=-1)
            out = jnp.einsum('bhwij,bhwjd->bhwid', attn, bv)
            return out.reshape(b, h, n, d)

        def _layer(x, wqkv, qs, ksc, wo, lg, lb, w1, b1, w2, b2):
            b, n, _ = x.shape
            h = shift_token(x)
            qkv = h @ wqkv
            q, k, v = jnp.split(qkv, 3, axis=-1)
            to_heads = lambda t: t.reshape(b, n, HEADS, DIM_HEAD).transpose(0, 2, 1, 3)
            q, k, v = (to_heads(q), to_heads(k), to_heads(v))
            q = l2norm(q) * qs
            k = l2norm(k) * ksc
            q, k = rotary_xpos(q, k)
            o = local_attention(q, k, v)
            o = o.transpose(0, 2, 1, 3).reshape(b, n, INNER)
            x = x + o @ wo
            h = shift_token(x)
            mu = h.mean(-1, keepdims=True)
            var = h.var(-1, keepdims=True)
            h = (h - mu) / jnp.sqrt(var + 1e-05) * lg + lb
            h = h @ w1 + b1
            a, g = jnp.split(h, 2, axis=-1)
            h = a * jax.nn.gelu(g, approximate=False)
            x = x + h @ w2 + b2
            return x
        key = jax.random.key(seed)
        ks = jax.random.split(key, 6)
        return {'x': jax.random.normal(ks[0], (B, N, DIM), jnp.float32), 'wqkv': jax.random.normal(ks[1], (DEPTH, DIM, 3 * INNER), jnp.float32) * 0.02, 'q_scale': jnp.ones((DEPTH, DIM_HEAD), jnp.float32), 'k_scale': jnp.ones((DEPTH, DIM_HEAD), jnp.float32), 'wo': jax.random.normal(ks[2], (DEPTH, INNER, DIM), jnp.float32) * 0.02, 'ln_g': jnp.ones((DEPTH, DIM), jnp.float32), 'ln_b': jnp.zeros((DEPTH, DIM), jnp.float32), 'w1': jax.random.normal(ks[3], (DEPTH, DIM, 2 * HID), jnp.float32) * 0.02, 'b1': jnp.zeros((DEPTH, 2 * HID), jnp.float32), 'w2': jax.random.normal(ks[4], (DEPTH, HID, DIM), jnp.float32) * 0.02, 'b2': jnp.zeros((DEPTH, DIM), jnp.float32)}
    _L0_ffn_in = _L0_ffn_setup()
    _L0_c = _w((lambda *s: np.random.randn(*s).astype(np.float32) * 0.05)(16, 128))
    _L0_wmod = _w((lambda *s: np.random.randn(*s).astype(np.float32) * 0.05)(128, 6 * 128) * 128 ** (-0.5))
    _d = {'L0_attn_embeddings': _L0_attn_in['embeddings'], 'L0_attn_guidance_trajectories': _L0_attn_in['guidance_trajectories'], 'L0_ffn_wqkv': _L0_ffn_in['wqkv'], 'L0_ffn_q_scale': _L0_ffn_in['q_scale'], 'L0_ffn_k_scale': _L0_ffn_in['k_scale'], 'L0_ffn_wo': _L0_ffn_in['wo'], 'L0_ffn_ln_g': _L0_ffn_in['ln_g'], 'L0_ffn_ln_b': _L0_ffn_in['ln_b'], 'L0_ffn_w1': _L0_ffn_in['w1'], 'L0_ffn_b1': _L0_ffn_in['b1'], 'L0_ffn_w2': _L0_ffn_in['w2'], 'L0_ffn_b2': _L0_ffn_in['b2'], 'L0_c': _L0_c, 'L0_wmod': _L0_wmod}
    _x0 = _d['L0_attn_embeddings']
    _d['L0_attn_embeddings'] = jax.random.normal(jax.random.fold_in(jax.random.key(seed), 1), (16, 256, 128), dtype=_x0.dtype)
    del _x0
    return _d

def reference(L0_attn_embeddings, L0_attn_guidance_trajectories, L0_ffn_wqkv, L0_ffn_q_scale, L0_ffn_k_scale, L0_ffn_wo, L0_ffn_ln_g, L0_ffn_ln_b, L0_ffn_w1, L0_ffn_b1, L0_ffn_w2, L0_ffn_b2, L0_c, L0_wmod):

    def _L0_attn_ref(embeddings, guidance_trajectories):
        import jax, jax.numpy as jnp
        import numpy as np
        MAX_DIST = 8
        GUIDANCE_WEIGHT = 0.4
        EPS_MAG = 1e-06
        EPS_COS = 1e-08
        EPS_WSUM = 1e-08
        B, S, D = embeddings.shape
        W = min(MAX_DIST, S - 1)
        diffs = embeddings[:, 1:, :] - embeddings[:, :-1, :]
        pos = jnp.arange(S)[:, None]
        k = jnp.arange(W)[None, :]
        idx = pos - W + k
        valid = (idx >= 0) & (pos >= 1)
        windows = diffs[:, jnp.clip(idx, 0, S - 2), :]
        w = jnp.minimum(pos, W)
        j = k - (W - w)
        lin = jnp.where(w > 1, 0.1 + 0.9 * j / jnp.maximum(w - 1, 1), 0.1)
        pos_weights = jnp.where(valid, lin, 0.0).astype(embeddings.dtype)
        mag = jnp.linalg.norm(windows, axis=-1, keepdims=True)
        is_valid_mag = mag > EPS_MAG
        normed = jnp.where(is_valid_mag, windows / jnp.where(is_valid_mag, mag, 1.0), 0.0)
        mag_weights = jnp.tanh(mag * 2.0)
        combined = pos_weights[None, :, :, None] * mag_weights
        g_norm = jnp.linalg.norm(guidance_trajectories, axis=-1)
        a_norm = jnp.linalg.norm(normed, axis=-1)
        dots = jnp.einsum('bswd,gd->bswg', normed, guidance_trajectories)
        sims = dots / (jnp.maximum(a_norm, EPS_COS)[..., None] * jnp.maximum(g_norm, EPS_COS))
        g_weights = jax.nn.softmax(sims * 2.0, axis=-1)
        influence = jnp.einsum('bswg,gd->bswd', g_weights, guidance_trajectories)
        blended = (1.0 - GUIDANCE_WEIGHT) * normed + GUIDANCE_WEIGHT * influence
        weight_sum = jnp.maximum(combined.sum(axis=2), EPS_WSUM)
        trajectories = (blended * combined).sum(axis=2) / weight_sum
        return trajectories

    def _L0_ffn_ref(x, wqkv, q_scale, k_scale, wo, ln_g, ln_b, w1, b1, w2, b2):
        import jax, jax.numpy as jnp
        import numpy as np
        DIM = 128
        DEPTH = 2
        HEADS = 8
        DIM_HEAD = 64
        WINDOW = 64
        INNER = HEADS * DIM_HEAD
        HID = int(DIM * 4 * 2 / 3)
        B, N = (2, 1024)
        QK_SCALE = 8.0

        def shift_token(t):
            t1, t2 = jnp.split(t, 2, axis=-1)
            t2 = jnp.pad(t2, ((0, 0), (1, 0), (0, 0)))[:, :-1]
            return jnp.concatenate([t1, t2], axis=-1)

        def l2norm(t):
            return t / jnp.clip(jnp.linalg.norm(t, axis=-1, keepdims=True), 1e-12)

        def rotate_half(x):
            x1, x2 = jnp.split(x, 2, axis=-1)
            return jnp.concatenate([-x2, x1], axis=-1)

        def rotary_xpos(q, k):
            n = q.shape[-2]
            half_idx = jnp.arange(0, DIM_HEAD, 2, dtype=jnp.float32)
            inv_freq = 1.0 / 10000.0 ** (half_idx / DIM_HEAD)
            t = jnp.arange(n, dtype=jnp.float32)
            freqs = t[:, None] * inv_freq[None, :]
            freqs = jnp.concatenate([freqs, freqs], axis=-1)
            base = (half_idx + 0.4 * DIM_HEAD) / (1.4 * DIM_HEAD)
            power = (t - n // 2) / float(WINDOW // 2)
            scale = base[None, :] ** power[:, None]
            scale = jnp.concatenate([scale, scale], axis=-1)
            cos, sin = (jnp.cos(freqs), jnp.sin(freqs))
            q = q * cos * scale + rotate_half(q) * sin * scale
            k = k * cos / scale + rotate_half(k) * sin / scale
            return (q, k)

        def local_attention(q, k, v):
            b, h, n, d = q.shape
            w = n // WINDOW
            bq = q.reshape(b, h, w, WINDOW, d) * QK_SCALE
            bk = k.reshape(b, h, w, WINDOW, d)
            bv = v.reshape(b, h, w, WINDOW, d)

            def look_around(t):
                p = jnp.pad(t, ((0, 0), (0, 0), (1, 0), (0, 0), (0, 0)))
                return jnp.concatenate([p[:, :, :w], p[:, :, 1:]], axis=3)
            bk, bv = (look_around(bk), look_around(bv))
            bt = jnp.arange(n).reshape(w, WINDOW)
            btp = jnp.pad(bt, ((1, 0), (0, 0)), constant_values=-1)
            btk = jnp.concatenate([btp[:w], btp[1:]], axis=1)
            sim = jnp.einsum('bhwid,bhwjd->bhwij', bq, bk)
            i = bt[:, :, None]
            j = btk[:, None, :]
            mask = (i < j) | (i > j + WINDOW) | (j == -1)
            sim = jnp.where(mask, -jnp.finfo(sim.dtype).max, sim)
            attn = jax.nn.softmax(sim, axis=-1)
            out = jnp.einsum('bhwij,bhwjd->bhwid', attn, bv)
            return out.reshape(b, h, n, d)

        def _layer(x, wqkv, qs, ksc, wo, lg, lb, w1, b1, w2, b2):
            b, n, _ = x.shape
            h = shift_token(x)
            qkv = h @ wqkv
            q, k, v = jnp.split(qkv, 3, axis=-1)
            to_heads = lambda t: t.reshape(b, n, HEADS, DIM_HEAD).transpose(0, 2, 1, 3)
            q, k, v = (to_heads(q), to_heads(k), to_heads(v))
            q = l2norm(q) * qs
            k = l2norm(k) * ksc
            q, k = rotary_xpos(q, k)
            o = local_attention(q, k, v)
            o = o.transpose(0, 2, 1, 3).reshape(b, n, INNER)
            x = x + o @ wo
            h = shift_token(x)
            mu = h.mean(-1, keepdims=True)
            var = h.var(-1, keepdims=True)
            h = (h - mu) / jnp.sqrt(var + 1e-05) * lg + lb
            h = h @ w1 + b1
            a, g = jnp.split(h, 2, axis=-1)
            h = a * jax.nn.gelu(g, approximate=False)
            x = x + h @ w2 + b2
            return x
        for l in range(DEPTH):
            x = _layer(x, wqkv[l], q_scale[l], k_scale[l], wo[l], ln_g[l], ln_b[l], w1[l], b1[l], w2[l], b2[l])
        return x
    x = L0_attn_embeddings
    mod = (_silu(L0_c) @ L0_wmod).reshape(L0_c.shape[0], 6, 1, -1)
    sa, ca, ga, sb, cb, gb = (mod[:, 0], mod[:, 1], mod[:, 2], mod[:, 3], mod[:, 4], mod[:, 5])
    ga = (2 * (ga >= 0) - 1) * jnp.maximum(jnp.abs(ga), 0.25)
    gb = (2 * (gb >= 0) - 1) * jnp.maximum(jnp.abs(gb), 0.25)
    h = _layernorm(x, axis=-1) * (1 + ca) + sa
    x = x + ga * _L0_attn_ref(h, L0_attn_guidance_trajectories)
    h = _layernorm(x, axis=-1) * (1 + cb) + sb
    x = x + gb * _L0_ffn_ref(h, L0_ffn_wqkv, L0_ffn_q_scale, L0_ffn_k_scale, L0_ffn_wo, L0_ffn_ln_g, L0_ffn_ln_b, L0_ffn_w1, L0_ffn_b1, L0_ffn_w2, L0_ffn_b2)
    return x

_drawn_inputs = setup_inputs


def setup_inputs(seed=0):
    import zlib

    import numpy as np

    out = dict(_drawn_inputs(seed))
    spreads = {'L0_ffn_q_scale': (1.0, 0.6),
     'L0_ffn_k_scale': (1.0, 0.6),
     'L0_ffn_ln_g': (1.0, 0.6),
     'L0_ffn_ln_b': (0.0, 0.8),
     'L0_ffn_b1': (0.0, 0.8),
     'L0_ffn_b2': (0.0, 0.775)}
    factors = {'L0_attn_guidance_trajectories': 4.43,
     'L0_ffn_wqkv': 6.937,
     'L0_ffn_wo': 6.956,
     'L0_ffn_w1': 8.0,
     'L0_ffn_w2': 8.0}
    for name, (base, spread) in spreads.items():
        noise = np.random.default_rng([zlib.crc32(name.encode()), seed]).standard_normal(out[name].shape)
        drawn = base * np.exp(spread * noise) if base else spread * noise
        out[name] = jnp.asarray(drawn.astype(out[name].dtype))
    for name, factor in factors.items():
        out[name] = (out[name] * factor).astype(out[name].dtype)
    return out
```

```python
from contextlib import ExitStack

import concourse.bass as bass
from concourse import mybir

F32 = mybir.dt.float32
F32R = mybir.dt.float32r
BF16 = mybir.dt.bfloat16
I32 = mybir.dt.int32
ALU = mybir.AluOpType
ACT = mybir.ActivationFunctionType
AX_X = mybir.AxisListType.X

P = 128
SEQ = 256
TILES = 4
UNIT = TILES * P
HEADS, DH, WIN = 8, 64, 64
INNER = HEADS * DH
HID = int(P * 4 * 2 / 3)
HID_CHUNKS = [(0, 128), (128, 128), (256, HID - 256)]
GUIDES = 64
DEPTH = 2
QKV = 3 * INNER
GUIDANCE = 0.4
VW = DH + 1
WEIGHED = P + 1 + GUIDES
VS = P + 2
RSQRT_SEED = float(0x5F3759DF - (1 << 22))
NEWTON = 11

ROW_LN_G, ROW_LN_B, ROW_B2, ROW_B1 = 0, DEPTH, 2 * DEPTH, 3 * DEPTH
N_ROWS = ROW_B1 + 6 * DEPTH
MOD_SA, MOD_CA, MOD_GA, MOD_SB, MOD_CB, MOD_GB = range(6)

FF, NEW, PROJ, STORE = "ff", "new", "proj", "store"

ORDER_LATE = [
    ("a", "turn", 0), (FF, "stats"), ("a", "score", 0), ("a", "turn", 1), (FF, "norm"), ("a", "score", 1),
    ("a", "flip", 0), (FF, "up", 0), ("a", "mix", 0), (FF, "up", 1), ("a", "out", 0),
    ("a", "turn", 2), (FF, "up", 2), ("a", "score", 2), (FF, "down"),
    ("a", "flip", 1), ("a", "mix", 1), (PROJ, "split"), ("a", "out", 1), ("a", "turn", 3), (PROJ, "tile", 0),
    ("a", "score", 3), (PROJ, "tile", 1), ("a", "flip", 2), ("a", "mix", 2), (PROJ, "rsqrt", 0), ("a", "out", 2),
    (PROJ, "tile", 2), ("a", "flip", 3), ("a", "mix", 3), (PROJ, "unit", 0), (PROJ, "tile", 3), ("a", "out", 3),
    (PROJ, "rsqrt", 1), ("a", "project"), (PROJ, "unit", 1),
]
ORDER_EARLY = [
    (NEW, "stats"), ("a", "turn", 0), (FF, "stats"), ("a", "score", 0), (NEW, "turn"), ("a", "turn", 1), (FF, "norm"),
    (NEW, "steps"), ("a", "score", 1), (NEW, "dots"), ("a", "flip", 0), (NEW, "sims"), ("a", "mix", 0),
    (NEW, "weights"), ("a", "out", 0), (FF, "up", 0), (NEW, "mix"), (FF, "up", 1),
    ("a", "turn", 2), (FF, "up", 2), ("a", "score", 2), (FF, "down"), (STORE, "scale"),
    ("a", "flip", 1), (STORE, "turn"), (NEW, "sum"), (NEW, "gate"), ("a", "mix", 1), ("a", "out", 1), (NEW, "stream"),
    ("a", "turn", 3), (PROJ, "split"), ("a", "score", 3), (PROJ, "tile", 0),
    (PROJ, "tile", 1), ("a", "flip", 2), ("a", "mix", 2), (PROJ, "rsqrt", 0), ("a", "out", 2),
    (PROJ, "tile", 2), ("a", "flip", 3), ("a", "mix", 3), (PROJ, "unit", 0), (PROJ, "tile", 3), ("a", "out", 3),
    (PROJ, "rsqrt", 1), ("a", "project"), (PROJ, "unit", 1),
]
ORDER = [ORDER_EARLY, ORDER_EARLY, ORDER_LATE, ORDER_LATE]

BANKS_OF = {(FF, "stats"): 1, (FF, "norm"): 1, (FF, "up"): 2, (FF, "down"): 1, (STORE, "turn"): 1,
            (NEW, "turn"): 1, (NEW, "dots"): 2, (NEW, "mix"): 1, (NEW, "sum"): 2, (NEW, "stream"): 1,
            (PROJ, "tile"): 3}
DENSE_BANKS = 3


def runs(i, slot, step, turns):
    kind = step[0]
    if isinstance(i, int) and i == 0:
        return not (slot < 2 and kind in (FF, STORE)) and not (kind == "a" and slot == 0)
    if isinstance(i, int) and i == turns:
        return slot < 2 and (kind in (FF, STORE) or (kind == "a" and slot == 0))
    return True


class BankTurns:

    def __init__(self, turns):
        self.turns = turns
        self.bank = {}
        place = 0
        self.steps = []
        for slot in range(4):
            for step in ORDER[slot]:
                for n in range(BANKS_OF.get(step[:2], 0) if step[0] != "a" else 0):
                    self.bank[(slot, step, n)] = place % DENSE_BANKS
                    self.steps.append((slot, step, n))
                    place += 1

    def before(self, i, key):
        count = 0
        for other in self.steps:
            if other == key:
                break
            if self.bank[other] == self.bank[key] and runs(i, other[0], other[1], self.turns):
                count += 1
        return count

    def whole(self, i, bank):
        return sum(self.bank[k] == bank and runs(i, k[0], k[1], self.turns) for k in self.steps)

    def of(self, i, slot, step, n=0):
        key = (slot, step, n)
        bank = self.bank[key]
        if isinstance(i, int) and i == 0:
            return bank, self.before(0, key)
        first, full = self.whole(0, bank), self.whole(None, bank)
        if isinstance(i, int):
            return bank, first + (i - 1) * full + self.before(i, key)
        return bank, i * full + (first - full + self.before(None, key))


def past(count):
    return not isinstance(count, int) or count > 0


def adaln_block(nc, x, traj, wqkv, q_scale, k_scale, wo, ln_g, ln_b, w1, b1, w2, b2, c, wmod,
                eye, masks, band, rotary, out):
    n_seq = x.shape[0]
    units = n_seq * SEQ // UNIT
    turns = units // 2
    bank_turns = BankTurns(turns)

    with ExitStack() as ctx:
        def sb(name, shape, dt=F32):
            return ctx.enter_context(nc.sbuf_tensor(name, shape, dt))

        def sem(name):
            return ctx.enter_context(nc.semaphore(name))

        dense = [ctx.enter_context(nc.psum_tensor(f"dense{k}", [P, 512], F32)) for k in range(DENSE_BANKS)]
        pair = [[ctx.enter_context(nc.psum_tensor(f"pair{k}{m}", [P, 512], F32)) for m in range(2)] for k in range(2)]
        mixed = ctx.enter_context(nc.psum_tensor("mixed", [P, 512], F32))

        eye_s = sb("eye_s", [P, P])
        eye_h = sb("eye_h", [P, P], BF16)
        mask_h = sb("mask_h", [P, 2, 4, P], BF16)
        band_s = sb("band_s", [P, 2, SEQ])
        tables = sb("tables", [P, DEPTH, 2, 4, DH])
        three_halves = sb("three_halves", [P, 32])
        columns = sb("columns", [P, N_ROWS])
        guides = sb("guides", [GUIDES, P])
        dots_by = sb("dots_by", [P, GUIDES + P])
        mod = sb("mod", [P, 6, n_seq])
        gate_a = sb("gate_a", [P, n_seq, P])
        wq_hi, wq_lo = sb("wq_hi", [P, DEPTH, QKV], F32R), sb("wq_lo", [P, DEPTH, QKV], F32R)
        w1_hi, w1_lo = sb("w1_hi", [P, DEPTH, 2 * HID], F32R), sb("w1_lo", [P, DEPTH, 2 * HID], F32R)
        wo_s = sb("wo_s", [P, DEPTH, 4, P])
        w2_s = sb("w2_s", [P, DEPTH, 3, P])

        x_in = [sb(f"x_in{s}", [P, TILES, P]) for s in range(2)]
        x_mid = [sb(f"x_mid{s}", [P, TILES, P]) for s in range(2)]
        y_t = [sb(f"y_t{s}", [P, 2, SEQ]) for s in range(2)]
        qk = [sb(f"qk{s}", [P, TILES, 2 * INNER]) for s in range(2)]
        v = [sb(f"v{s}", [P, TILES, HEADS, VW]) for s in range(2)]
        v_cross = [sb(f"v_cross{s}", [P, 2, HEADS, VW]) for s in range(2)]

        xn = sb("xn", [P, TILES, P])
        h_a = sb("h_a", [P, 2, SEQ])
        step_t = sb("step_t", [P, 2, SEQ])
        shifted = sb("shifted", [P, 2, SEQ])
        hn = sb("hn", [P, UNIT])
        h_hi, h_lo = sb("h_hi", [P, UNIT], F32R), sb("h_lo", [P, UNIT], F32R)
        result = sb("result", [P, TILES, P])
        squares = sb("squares", [P, 2, UNIT])
        guide_mix = squares[0:GUIDES, 0, :]
        space = sb("space", [P, 8 * UNIT])
        turned_c = space[:, 0:4 * UNIT].rearrange("p (t m n) -> p t m n", t=2, m=2)
        turned_s = space[:, 4 * UNIT:].rearrange("p (t m n) -> p t m n", t=2, m=2)
        gelu = space[:, 0:2 * UNIT].rearrange("p (c n) -> p c n", c=2)
        hidden = space[:, 2 * UNIT:5 * UNIT].rearrange("p (c n) -> p c n", c=3)
        weighed = space[:, 5 * UNIT:5 * UNIT + TILES * WEIGHED].rearrange("p (t n) -> p t n", t=TILES)
        expd = space[:, 7 * UNIT:7 * UNIT + TILES * GUIDES].rearrange("p (t n) -> p t n", t=TILES)

        q_t = sb("q_t", [P, 2, 4, P])
        k_t = sb("k_t", [P, 4, 2 * P])
        probs = sb("probs", [P, 4, 4, P])
        probs_t = sb("probs_t", [P, 4, 4, P])
        o_rows = sb("o_rows", [P, 2, INNER])
        o_t = sb("o_t", [P, 4, UNIT])

        moments = sb("moments", [P, TILES, 6])
        mean_var = sb("mean_var", [P, TILES, 2])
        half, root, scratch = sb("half", [P, 32]), sb("root", [P, 32]), sb("scratch", [P, 32])
        half_f, root_f, scratch_f = sb("half_f", [P, 4]), sb("root_f", [P, 4]), sb("scratch_f", [P, 4])
        moments_f = sb("moments_f", [P, TILES, 6])
        mean_var_f = sb("mean_var_f", [P, TILES, 2])
        half_n, root_n, scratch_n = sb("half_n", [P, 4]), sb("root_n", [P, 4]), sb("scratch_n", [P, 4])
        q_norm = sb("q_norm", [P, 32])
        col = sb("col", [P, 16, 4])
        (SS, MAG, RM, AN, ANM, RAN, F_SIM, BIAS, DMAX, TANH, SUM_E, RSUM_E, CW, CN, WS, RWS) = range(16)
        spare = sb("spare", [P, 1])
        neg_max = sb("neg_max", [P, 4, 4])
        sum_p = sb("sum_p", [P, 2, 4])

        stage_q = qk[0][:, :, :].rearrange("p t n -> p (t n)")[:, 0:DEPTH * QKV].rearrange("p (l n) -> p l n", l=DEPTH)
        stage_1 = qk[1][:, :, :].rearrange("p t n -> p (t n)")[:, 0:DEPTH * 2 * HID].rearrange("p (l n) -> p l n", l=DEPTH)
        wmod_s = o_t[:, :, :].rearrange("p k n -> p (k n)")[:, 0:6 * P]
        gate_wide = probs_t[:, :, :, :].rearrange("p a k n -> p (a k) n")[:, 0:n_seq, :]
        places = probs[:, :, :, :].rearrange("p a k n -> p (a k n)")
        rotary_s = places[:, 0:8 * DH].rearrange("p (t w d) -> p t w d", t=2, w=4)
        scales_s = places[:, 8 * DH:12 * DH].rearrange("p (l m d) -> p l m d", l=DEPTH, m=2)
        masks_s = places[:, 12 * DH:12 * DH + 2 * P].rearrange("p (t n) -> p t n", t=2)
        vectors = places[0:N_ROWS, 1024:1024 + P]
        crow = places[0:n_seq, 1152:1152 + P]
        gnorm = places[0:GUIDES, 1280:1280 + P]
        silu_t = places[:, 1408:1408 + n_seq]
        sign = places[:, 1536:1536 + n_seq]

        const_in, w_in, wo_in, rows_in, table_in = sem("const_in"), sem("w_in"), sem("wo_in"), sem("rows_in"), sem("table_in")
        rows_cleared, setup_self = sem("rows_cleared"), sem("setup_self")
        setup_pe, setup_act, setup_dve, setup_pool = (
            sem("setup_pe"), sem("setup_act"), sem("setup_dve"), sem("setup_pool"))
        weights_ready = sem("weights_ready")
        filled = [sem(f"filled{k}") for k in range(DENSE_BANKS)]
        emptied = [sem(f"emptied{k}") for k in range(DENSE_BANKS)]
        x_loaded, x_used, stored = [sem("x_loaded0"), sem("x_loaded1")], [sem("x_used0"), sem("x_used1")], sem("stored")
        ff_shifted, ff_self, ff_seeded, ff_rooted = sem("ff_shifted"), sem("ff_self"), sem("ff_seeded"), sem("ff_rooted")
        ff_newton, new_newton, qk_newton = sem("ff_newton"), sem("new_newton"), sem("qk_newton")
        ff_hi, ff_lo = sem("ff_hi"), sem("ff_lo")
        new_self, new_seeded, new_rooted, new_normed = sem("new_self"), sem("new_seeded"), sem("new_rooted"), sem("new_normed")
        new_steps, new_squares, new_exp = sem("new_steps"), sem("new_squares"), sem("new_exp")
        new_sims, new_weighed = sem("new_sims"), sem("new_weighed")
        qkv_shifted, qkv_hi, qkv_lo = sem("qkv_shifted"), sem("qkv_hi"), sem("qkv_lo")
        squared, summed, rotated, added = sem("squared"), sem("summed"), sem("rotated"), sem("added")
        qk_self, qk_seeded, qk_rooted, qk_ready = sem("qk_self"), sem("qk_seeded"), sem("qk_rooted"), sem("qk_ready")
        final_scaled = sem("final_scaled")
        turned, kept, scored, maxed = sem("turned"), sem("kept"), sem("scored"), sem("maxed")
        exped, flipped, flip_kept = sem("exped"), sem("flipped"), sem("flip_kept")
        mixed_full, mix_self, mix_normed = sem("mixed_full"), sem("mix_self"), sem("mix_normed")
        out_turned, out_kept, projected, attended = sem("out_turned"), sem("out_kept"), sem("projected"), sem("attended")

        def att(i, slot):
            return [(1, 1, i * 4 - 1), (0, 0, i * 4), (1, 0, i * 4 + 1), (0, 1, i * 4 + 2)][slot]

        def stream(slot):
            return slot % 2

        def ff(i, slot):
            return [(1, i * 4 - 2, i * 4 - 1), (1, i * 4 - 1, i * 4), (0, i * 4, i * 4 + 1), (0, i * 4 + 1, i * 4 + 2)][slot]

        def new(i, slot):
            return i * 2 + slot

        def proj(i, slot):
            return (0 if slot < 2 else 1), i * 4 + slot

        def bank(i, slot, step, n=0):
            return dense[bank_turns.of(i, slot, step, n)[0]]

        def filled_at(i, slot, step, n=0):
            b, before = bank_turns.of(i, slot, step, n)
            return filled[b], before + 1

        def read_at(i, slot, step, n=0):
            b, before = bank_turns.of(i, slot, step, n)
            return emptied[b], before + 1

        def read_before(i, slot, step, n=0):
            b, before = bank_turns.of(i, slot, step, n)
            return emptied[b], before

        def refilled(i, slot, step, n=0):
            return past(bank_turns.of(i, slot, step, n)[1])

        def empty(i, slot, step, n=0):
            return emptied[bank_turns.of(i, slot, step, n)[0]]

        def every_turn(eng, take):
            def turn(i):
                for slot in range(4):
                    for step in ORDER[slot]:
                        if runs(i, slot, step, turns):
                            take(i, slot, step)
            turn(0)
            with eng.Fori(1, turns) as i:
                turn(i)
            turn(turns)

        def rot(layer, t, which):
            row = tables[:, layer, t % 2, which, :].rearrange("p (o a b) -> p o a b", o=1, a=2)
            return row.broadcast_to([P, HEADS, 2, DH // 2])

        ROW_LOADS = 3 + 4 * DEPTH

        def flat(tile):
            return tile[:, :, :].rearrange("p a b -> p (a b)")

        def of_seq(row, i, slot, b):
            at = i * 4 + 2 * stream(slot) + b
            return mod[:, row, at:at + 1] if isinstance(i, int) else mod[:, row, bass.ds(at, 1)]

        block = ctx.enter_context(nc.Block())

        @block.sync
        def _(sp):
            def load_x(i, s):
                seqs = x[bass.ds(i * 4 + 2 * s, 2)] if not isinstance(i, int) else x[i * 4 + 2 * s:i * 4 + 2 * s + 2]
                sp.dma_start(x_in[s][:, :, :], seqs.rearrange("b (t p) d -> p (b t) d", p=P)).then_inc(x_loaded[s], 16)

            sp.dma_start(eye_s[:, :], eye).then_inc(const_in, 16)
            sp.dma_start(crow, c).then_inc(const_in, 16)
            sp.dma_start(wmod_s, wmod).then_inc(const_in, 16)
            sp.dma_start(guides[:, :], traj).then_inc(const_in, 16)
            load_x(0, 0)
            sp.dma_start(rotary_s, rotary).then_inc(table_in, 16)
            sp.dma_start(masks_s, masks).then_inc(table_in, 16)
            sp.dma_start(scales_s[:, :, 0, :], q_scale.partition_broadcast(P)).then_inc(table_in, 16)
            sp.dma_start(scales_s[:, :, 1, :], k_scale.partition_broadcast(P)).then_inc(table_in, 16)
            sp.wait_ge(rows_cleared, 1)
            for row, rows in ((ROW_LN_G, ln_g), (ROW_LN_B, ln_b), (ROW_B2, b2)):
                sp.dma_start(vectors[row:row + DEPTH, :], rows).then_inc(rows_in, 16)
            for l in range(DEPTH):
                for m in range(2):
                    row = ROW_B1 + 6 * l + 3 * m
                    sp.dma_start(vectors[row:row + 2, :],
                                 b1[l, m * HID:m * HID + 2 * P].rearrange("(c p) -> c p", p=P)).then_inc(rows_in, 16)
                    sp.dma_start(vectors[row + 2:row + 3, 0:HID - 2 * P],
                                 b1[l:l + 1, m * HID + 2 * P:(m + 1) * HID]).then_inc(rows_in, 16)
            sp.dma_start(stage_q, wqkv.rearrange("l d n -> d l n")).then_inc(w_in, 16)
            sp.dma_start(stage_1, w1.rearrange("l d n -> d l n")).then_inc(w_in, 16)
            sp.dma_start(band_s[:, :, :], band).then_inc(stored, 16)
            load_x(0, 1)
            for l in range(DEPTH):
                sp.dma_start(wo_s[:, l, :, :], wo[l].rearrange("(c p) d -> p c d", p=P)).then_inc(wo_in, 16)
                sp.dma_start(w2_s[:, l, 0:2, :], w2[l, 0:2 * P].rearrange("(c p) d -> p c d", p=P)).then_inc(wo_in, 16)
                sp.dma_start(w2_s[0:HID - 2 * P, l, 2, :], w2[l, 2 * P:HID]).then_inc(wo_in, 16)

            def take(i, slot, step):
                s = stream(slot)
                if step == (STORE, "turn"):
                    sp.wait_ge(*read_at(i, slot, step))
                    at = (i - 1) * 4 + 2 * s
                    seqs = out[bass.ds(at, 2)] if not isinstance(i, int) else out[at:at + 2]
                    sp.dma_start(seqs.rearrange("b (t p) d -> p (b t) d", p=P), result[:, :, :]).then_inc(stored, 16)

            def turn(i, last):
                for slot in range(4):
                    for step in ORDER[slot]:
                        if not runs(i, slot, step, turns):
                            continue
                        take(i, slot, step)
                        if step == (NEW, "gate") and not last:
                            sp.wait_ge(x_used[stream(slot)], i + 1)
                            load_x(i + 1, stream(slot))
            turn(0, False)
            if turns > 2:
                with sp.Fori(1, turns - 1) as i:
                    turn(i, False)
            with sp.Fori(turns - 1, turns) as i:
                turn(i, True)
            turn(turns, True)
            sp.wait_ge(stored, 16 * (units + 1))

        @block.tensor
        def _(pe):
            def done(ins, i, slot, step, n=0):
                ins.then_inc(filled[bank_turns.of(i, slot, step, n)[0]], 1)

            def turn_four(to, rows, own=False):
                for k in range(4):
                    last = pe.transpose(to[:, k * P:(k + 1) * P], rows(k), eye_s[:, :])
                return last

            pe.wait_ge(const_in, 64)
            pe.wait_ge(setup_act, 1)
            pe.transpose(pair[0][0][:, 0:n_seq], crow, eye_s[0:n_seq, 0:n_seq]).then_inc(setup_pe, 1)
            pe.wait_ge(setup_dve, 1)
            pe.transpose(pair[0][1][:, 0:GUIDES], gnorm, eye_s[0:GUIDES, 0:GUIDES]).then_inc(setup_pe, 1)
            pe.wait_ge(rows_in, 16 * ROW_LOADS)
            pe.transpose(pair[1][0][:, 0:N_ROWS], vectors, eye_s[0:N_ROWS, 0:N_ROWS]).then_inc(setup_pe, 1)
            pe.wait_ge(setup_dve, 2)
            for m in range(6):
                last = pe.matmul(pair[1][1][:, m * n_seq:(m + 1) * n_seq], wmod_s[:, m * P:(m + 1) * P], silu_t,
                                 start=True, stop=True)
            last.then_inc(setup_pe, 1)
            pe.wait_ge(setup_dve, 3)
            for b in range(n_seq):
                to = [dense[0], dense[1], dense[2], mixed][b // 4]
                last = pe.matmul(to[:, (b % 4) * P:(b % 4 + 1) * P], gate_wide[:, b, :], eye_s[:, :], start=True, stop=True)
            last.then_inc(setup_pe, 1)
            pe.wait_ge(setup_dve, 4)
            pe.wait_ge(setup_pool, 1)
            pe.wait_ge(stored, 16)

            def attention(i, slot, step):
                s, layer, before = att(i, slot)
                what = step[1]
                if what == "project":
                    pe.wait_ge(out_kept, before * 4 + 4)
                    for k in range(4):
                        last = pe.matmul(mixed[:, :], wo_s[:, layer, k, :], o_t[:, k, :], start=(k == 0), stop=(k == 3))
                    last.then_inc(projected, 1)
                    return
                t = step[2]
                tau = before * 4 + t
                banks = pair[t % 2]
                if what == "turn":
                    pe.wait_ge(qk_ready, 2 * before + t // 2 + 1)
                    if past(tau - 1):
                        pe.wait_ge(out_kept, tau - 1)
                    if past(2 * tau - 2):
                        pe.wait_ge(flip_kept, 2 * tau - 2)
                    turn_four(banks[0], lambda k: qk[s][:, t, k * P:(k + 1) * P]).then_inc(turned, 1)
                    turn_four(banks[1], lambda k: qk[s][:, t, INNER + k * P:INNER + (k + 1) * P]).then_inc(turned, 1)
                elif what == "score":
                    pe.wait_ge(kept, 2 * tau + 2)
                    for m in range(2):
                        pe.matmul(banks[m][:, :], eye_h[:, :], mask_h[:, t % 2, :, :], start=True, stop=False,
                                  skip_group_check=True)
                    for hh in range(4):
                        for w in range(2):
                            for m in range(2):
                                rows = slice(DH * m, DH * (m + 1))
                                keys = k_t[rows, hh, :]
                                if t % 2:
                                    keys = keys[:, 0:P] if w else \
                                        keys.rearrange("p (a b) -> p a b", b=WIN)[:, 0:4:3, :]
                                else:
                                    keys = keys[:, P:2 * P] if w else keys[:, P:P + WIN]
                                n = WIN if (t % 2 == 0 and w == 0) else P
                                last = pe.matmul(banks[m][w * WIN:(w + 1) * WIN, hh * P:hh * P + n],
                                                 q_t[rows, t % 2, hh, w * WIN:(w + 1) * WIN], keys,
                                                 start=False, stop=True, skip_group_check=True)
                                if hh == 3 and w == 1:
                                    last.then_inc(scored, 1)
                elif what == "flip":
                    for m in range(2):
                        pe.wait_ge(exped, 2 * tau + m + 1)
                        turn_four(banks[m], lambda k: probs[:, 2 * (t % 2) + m, k, :]).then_inc(flipped, 1)
                elif what == "mix":
                    for m in range(2):
                        pe.wait_ge(flip_kept, 2 * tau + m + 1)
                        if past(2 * tau + m):
                            pe.wait_ge(mix_normed, 2 * tau + m)
                        if t == 0 and m == 0:
                            if past(before):
                                pe.wait_ge(attended, before)
                        if m == 0:
                            source = (i, slot - 1) if slot else (i - 1, 3)
                            pe.wait_ge(*read_at(*source, (PROJ, "tile", t), 2))
                        for hh in range(4):
                            head = 2 * hh + m
                            for w in range(2):
                                values = v_cross[s][:, t // 2, head, :] if (t % 2 and w == 0) else v[s][:, t, head, :]
                                last = pe.matmul(mixed[w * WIN:(w + 1) * WIN, hh * VW:(hh + 1) * VW],
                                                 probs_t[:, 2 * (t % 2) + m, hh, w * WIN:(w + 1) * WIN], values,
                                                 start=True, stop=True)
                        last.then_inc(mixed_full, 1)
                elif what == "out":
                    pe.wait_ge(mix_normed, 2 * tau + 2)
                    turn_four(banks[0], lambda k: o_rows[:, t % 2, k * P:(k + 1) * P]).then_inc(out_turned, 1)

            def split_product(to, w_hi, w_lo, h_cols):
                pe.matmul(to, w_hi, h_hi[:, h_cols], start=True, stop=False)
                pe.matmul(to, w_hi, h_lo[:, h_cols], start=False, stop=False)
                return pe.matmul(to, w_lo, h_hi[:, h_cols], start=False, stop=True)

            def feed_forward(i, slot, step):
                layer, before, _ = ff(i, slot)
                what = step[1]
                if what == "stats":
                    pe.wait_ge(ff_shifted, before + 1)
                    if refilled(i, slot, step):
                        pe.wait_ge(*read_before(i, slot, step))
                    to = bank(i, slot, step)
                    done(turn_four(to, lambda k: flat(shifted)[:, k * P:(k + 1) * P]),
                         i, slot, step)
                elif what == "norm":
                    pe.wait_ge(*read_at(i, slot, (FF, "stats")))
                    if refilled(i, slot, step):
                        pe.wait_ge(*read_before(i, slot, step))
                    to = bank(i, slot, step)
                    done(turn_four(to, lambda k: hn[:, k * P:(k + 1) * P]), i, slot, step)
                elif what == "up":
                    at, n = HID_CHUNKS[step[2]]
                    if step[2] == 0:
                        pe.wait_ge(ff_lo, before + 1)
                    for m, base in enumerate((HID, 0)):
                        if refilled(i, slot, step, m):
                            pe.wait_ge(*read_before(i, slot, step, m))
                        to = bank(i, slot, step, m)
                        cols = slice(base + at, base + at + n)
                        done(split_product(to[0:n, :], w1_hi[:, layer, cols], w1_lo[:, layer, cols], slice(0, UNIT)),
                             i, slot, step, m)
                elif what == "down":
                    pe.wait_ge(*read_at(i, slot, (FF, "up", 2), 1))
                    if refilled(i, slot, step):
                        pe.wait_ge(*read_before(i, slot, step))
                    to = bank(i, slot, step)
                    for k, (_, n) in enumerate(HID_CHUNKS):
                        last = pe.matmul(to[:, :], w2_s[0:n, layer, k, :], hidden[0:n, k, :], start=(k == 0), stop=(k == 2))
                    done(last, i, slot, step)

            def new_unit(i, slot, step):
                before = new(i, slot)
                what = step[1]
                if what == "turn":
                    pe.wait_ge(new_normed, 2 * before + 1)
                    if refilled(i, slot, step):
                        pe.wait_ge(*read_before(i, slot, step))
                    to = bank(i, slot, step)
                    done(turn_four(to, lambda k: xn[:, k, :]), i, slot, step)
                elif what == "dots":
                    pe.wait_ge(new_steps, before + 1)
                    for m in range(2):
                        if refilled(i, slot, step, m):
                            pe.wait_ge(*read_before(i, slot, step, m))
                        to = bank(i, slot, step, m)
                        for k in range(2):
                            j = 2 * m + k
                            last = pe.matmul(to[:, k * (GUIDES + P):(k + 1) * (GUIDES + P)],
                                             step_t[:, j // 2, (j % 2) * P:(j % 2 + 1) * P], dots_by[:, :],
                                             start=True, stop=True)
                        done(last, i, slot, step, m)
                elif what == "mix":
                    pe.wait_ge(new_weighed, before + 1)
                    if refilled(i, slot, step):
                        pe.wait_ge(*read_before(i, slot, step))
                    to = bank(i, slot, step)
                    for b in range(2):
                        pe.matmul(to[0:GUIDES, b * SEQ:(b + 1) * SEQ], weighed[:, 2 * b, P + 1:P + 1 + GUIDES],
                                  band_s[:, 0, :], start=True, stop=False, skip_group_check=True)
                        last = pe.matmul(to[0:GUIDES, b * SEQ + P:(b + 1) * SEQ], weighed[:, 2 * b + 1, P + 1:P + 1 + GUIDES],
                                         band_s[:, 1, P:SEQ], start=False, stop=True, skip_group_check=True)
                    done(last, i, slot, step)
                elif what == "sum":
                    pe.wait_ge(*read_at(i, slot, (NEW, "mix")))
                    for m in range(2):
                        if refilled(i, slot, step, m):
                            pe.wait_ge(*read_before(i, slot, step, m))
                        to = bank(i, slot, step, m)
                        for k in range(2):
                            o = to[:, k * VS:k * VS + P + 1]
                            pe.matmul(o, band_s[:, 0, k * P:(k + 1) * P], weighed[:, 2 * m, 0:P + 1], start=True,
                                      stop=False, skip_group_check=True)
                            if k:
                                pe.matmul(o, band_s[:, 1, P:SEQ], weighed[:, 2 * m + 1, 0:P + 1], start=False,
                                          stop=False, skip_group_check=True)
                            j = 2 * m + k
                            last = pe.matmul(to[:, k * VS:k * VS + P], guide_mix[:, j * P:(j + 1) * P], guides[:, :],
                                             start=False, stop=True, skip_group_check=True)
                        done(last, i, slot, step, m)
                elif what == "stream":
                    pe.wait_ge(new_normed, 2 * before + 2)
                    if refilled(i, slot, step):
                        pe.wait_ge(*read_before(i, slot, step))
                    to = bank(i, slot, step)
                    done(turn_four(to, lambda k: xn[:, k, :]), i, slot, step)

            def projections(i, slot, step):
                layer, before = proj(i, slot)
                if step[1] != "tile":
                    return
                t = step[2]
                if t == 0:
                    pe.wait_ge(qkv_lo, before + 1)
                    if isinstance(i, int) and i == 0 and slot == 0:
                        pe.wait_ge(weights_ready, 2)
                        pe.wait_ge(wo_in, 16 * 3 * DEPTH)
                rows = slice(t * P, (t + 1) * P)
                for m in range(3):
                    if refilled(i, slot, step, m):
                        pe.wait_ge(*read_before(i, slot, step, m))
                    to = bank(i, slot, step, m)
                    cols = slice(m * INNER, (m + 1) * INNER)
                    pe.matmul(to[:, :], h_hi[:, rows], wq_hi[:, layer, cols], start=True, stop=False)
                    pe.matmul(to[:, :], h_hi[:, rows], wq_lo[:, layer, cols], start=False, stop=False)
                    done(pe.matmul(to[:, :], h_lo[:, rows], wq_hi[:, layer, cols], start=False, stop=True), i, slot, step, m)

            def take(i, slot, step):
                if step[0] == "a":
                    attention(i, slot, step)
                elif step[0] == FF:
                    feed_forward(i, slot, step)
                elif step[0] == NEW:
                    new_unit(i, slot, step)
                elif step[0] == PROJ:
                    projections(i, slot, step)
                elif step == (STORE, "turn"):
                    pe.wait_ge(final_scaled, new(i, slot) - 1)
                    if refilled(i, slot, step):
                        pe.wait_ge(*read_before(i, slot, step))
                    to = bank(i, slot, step)
                    done(turn_four(to, lambda k: hn[:, k * P:(k + 1) * P]), i, slot, step)

            every_turn(pe, take)


        @block.scalar
        def _(act):
            act.wait_ge(const_in, 64)
            act.activation(crow, crow, ACT.Silu).then_inc(setup_act, 1)

            def attention(i, slot, step):
                s, layer, before = att(i, slot)
                if step[1] in ("project", "mix"):
                    return
                what, t = step[1:]
                tau = before * 4 + t
                banks = pair[t % 2]
                if what == "turn":
                    act.wait_ge(turned, 2 * tau + 1)
                    used = 2 * tau if t % 2 == 0 else 2 * tau - 2
                    if past(used):
                        act.wait_ge(scored, used)
                    act.activation(q_t[:, t % 2, :, :], banks[0][:, :].rearrange("p (k n) -> p k n", k=4),
                                   ACT.Copy).then_inc(kept, 1)
                    act.wait_ge(turned, 2 * tau + 2)
                    cols = slice(0, P) if t % 2 else slice(P, 2 * P)
                    act.activation(k_t[:, :, cols], banks[1][:, :].rearrange("p (k n) -> p k n", k=4),
                                   ACT.Copy).then_inc(kept, 1)
                elif what == "score":
                    for m in range(2):
                        ring = 2 * (t % 2) + m
                        act.wait_ge(maxed, 2 * tau + m + 1)
                        if past(2 * tau + m - 3):
                            act.wait_ge(flipped, 2 * tau + m - 3)
                        for hh in range(4):
                            last = act.activation(probs[:, ring, hh, :], banks[m][:, hh * P:(hh + 1) * P], ACT.Exp,
                                                  bias=neg_max[:, ring, hh:hh + 1], scale=1.0)
                        last.then_inc(exped, 1)
                elif what == "flip":
                    for m in range(2):
                        act.wait_ge(flipped, 2 * tau + m + 1)
                        if past(2 * tau + m - 3):
                            act.wait_ge(mixed_full, 2 * tau + m - 3)
                        act.activation(probs_t[:, 2 * (t % 2) + m, :, :],
                                       banks[m][:, :].rearrange("p (k n) -> p k n", k=4), ACT.Copy).then_inc(flip_kept, 1)
                elif what == "out":
                    act.wait_ge(out_turned, tau + 1)
                    if past(before):
                        act.wait_ge(projected, before)
                    act.activation(o_t[:, :, t * P:(t + 1) * P], banks[0][:, :].rearrange("p (k n) -> p k n", k=4),
                                   ACT.Copy).then_inc(out_kept, 1)

            def shift(s, done_sem):
                act.activation(shifted[0:P // 2, :, :], y_t[s][0:P // 2, :, :], ACT.Copy)
                act.activation(shifted[P // 2:P, :, 1:SEQ], y_t[s][P // 2:P, :, 0:SEQ - 1], ACT.Copy).then_inc(done_sem, 1)

            def feed_forward(i, slot, step):
                layer, before, att_upto = ff(i, slot)
                what = step[1]
                if what == "stats":
                    act.wait_ge(attended, att_upto)
                    used = proj(i, slot)[1] if not isinstance(i, int) or i < turns else 4 * turns
                    if past(used):
                        act.wait_ge(qkv_lo, used)
                    shift(stream(slot), ff_shifted)
                elif what == "norm":
                    act.wait_ge(*filled_at(i, slot, step))
                    src = bank(i, slot, step)
                    act.activation(hn[:, :], src[:, :], ACT.Identity, scale=columns[:, ROW_LN_G + layer:ROW_LN_G + layer + 1],
                                   bias=columns[:, ROW_LN_B + layer:ROW_LN_B + layer + 1]).then_inc(empty(i, slot, step), 1)
                elif what == "up":
                    chunk = step[2]
                    n = HID_CHUNKS[chunk][1]
                    act.wait_ge(*filled_at(i, slot, step, 0))
                    src = bank(i, slot, step, 0)
                    if chunk == 2:
                        act.wait_ge(*read_at(i, slot, (FF, "up", 0), 1))
                    row = ROW_B1 + 6 * layer + 3 + chunk
                    act.activation(gelu[0:n, chunk % 2, :], src[0:n, :], ACT.Gelu, bias=columns[0:n, row:row + 1],
                                   scale=1.0).then_inc(empty(i, slot, step, 0), 1)

            def new_unit(i, slot, step):
                before = new(i, slot)
                what = step[1]
                if what in ("turn", "stream"):
                    act.wait_ge(*filled_at(i, slot, step))
                    src = bank(i, slot, step)
                    add, scale = (MOD_SA, MOD_CA) if what == "turn" else (MOD_SB, MOD_CB)
                    to = h_a if what == "turn" else y_t[stream(slot)]
                    for b in range(2):
                        last = act.activation(to[:, b, :], src[:, b * SEQ:(b + 1) * SEQ], ACT.Identity,
                                              scale=of_seq(scale, i, slot, b), bias=of_seq(add, i, slot, b))
                    last.then_inc(empty(i, slot, step), 1)
                elif what == "dots":
                    for m in range(2):
                        act.wait_ge(*filled_at(i, slot, step, m))
                        src = bank(i, slot, step, m)
                        for k in range(2):
                            j = 2 * m + k
                            at = k * (GUIDES + P) + GUIDES
                            last = act.activation(weighed[:, j, 0:P], src[:, at:at + P], ACT.Square,
                                                  accum_out=col[:, SS, j:j + 1])
                    last.then_inc(new_squares, 1)
                elif what == "sims":
                    act.wait_ge(new_sims, before + 1)
                    act.activation(col[:, TANH, :], col[:, MAG, :], ACT.Tanh, scale=2.0)
                    for j in range(TILES):
                        at = (j % 2) * (GUIDES + P)
                        last = act.activation(expd[:, j, :], bank(i, slot, (NEW, "dots"), j // 2)[:, at:at + GUIDES], ACT.Exp,
                                              scale=col[:, F_SIM, j:j + 1], bias=col[:, BIAS, j:j + 1],
                                              accum_out=col[:, SUM_E, j:j + 1])
                    last.then_inc(new_exp, 1)
                elif what == "mix":
                    act.wait_ge(*filled_at(i, slot, step))
                    src = bank(i, slot, step)
                    act.activation(guide_mix, src[0:GUIDES, :], ACT.Copy).then_inc(empty(i, slot, step), 1)

            def projections(i, slot, step):
                layer, before = proj(i, slot)
                s = stream(slot)
                if step[1] == "split":
                    act.wait_ge(*read_at(i, slot, (NEW, "stream") if slot < 2 else (FF, "down")))
                    shift(s, qkv_shifted)
                elif step[1] == "tile":
                    t = step[2]
                    tau = 4 * before + t
                    for m in range(2):
                        act.wait_ge(*filled_at(i, slot, step, m))
                        src = bank(i, slot, step, m)
                        if past(2 * tau + m - 1):
                            act.wait_ge(summed, 2 * tau + m - 1)
                        act.activation(squares[:, m, :], src[:, :], ACT.Square).then_inc(squared, 1)
                    act.wait_ge(*filled_at(i, slot, step, 2))
                    src = bank(i, slot, step, 2)
                    half_rows = slice(0, WIN) if t % 2 else slice(WIN, P)
                    heads = src[:, :].rearrange("p (h d) -> p h d", h=HEADS)
                    act.activation(v_cross[s][half_rows, t // 2, :, 0:DH], heads[half_rows], ACT.Copy)
                    act.activation(v[s][:, t, :, 0:DH], heads, ACT.Copy).then_inc(empty(i, slot, step, 2), 1)

            def take(i, slot, step):
                if step[0] == "a":
                    attention(i, slot, step)
                elif step[0] == FF:
                    feed_forward(i, slot, step)
                elif step[0] == NEW:
                    new_unit(i, slot, step)
                elif step[0] == PROJ:
                    projections(i, slot, step)
                elif step == (STORE, "scale"):
                    act.wait_ge(*read_at(i, slot, (FF, "down")))
                    for b in range(2):
                        last = act.activation(hn[:, b * SEQ:(b + 1) * SEQ], y_t[stream(slot)][:, b, :], ACT.Copy,
                                              scale=of_seq(MOD_GB, i - 1, slot, b))
                    last.then_inc(final_scaled, 1)

            every_turn(act, take)

        @block.vector
        def _(dve):
            class Chain:

                def __init__(self, sem_, base):
                    self.sem, self.count = sem_, base

                def done(self, ins, fixed=False):
                    ins.then_inc(self.sem, 1)
                    self.count = self.count + 1
                    dve.wait_ge(self.sem, self.count)
                    if fixed:
                        dve.tensor_copy(spare[:, :], three_halves[:, 0:1])

            def rsqrt_seed(root_, half_, ins_sem):
                dve.tensor_scalar(root_.bitcast(I32), half_.bitcast(I32), -0.5, RSQRT_SEED, ALU.mult, ALU.add).then_inc(ins_sem, 1)

            dve.memset(vectors, 0.0).then_inc(rows_cleared, 1)
            own = Chain(setup_self, 0)
            dve.memset(three_halves[:, :], 1.5)
            dve.wait_ge(const_in, 64)
            g_half, g_root, g_tmp = half[0:GUIDES, 0:1], root[0:GUIDES, 0:1], scratch[0:GUIDES, 0:1]
            own.done(dve.tensor_tensor(gnorm, guides[:, :], guides[:, :], ALU.mult))
            own.done(dve.tensor_reduce(g_half, gnorm, AX_X, ALU.add))
            own.done(dve.tensor_scalar(g_half, g_half, 1e-16, 0.5, ALU.max, ALU.mult))
            own.done(dve.tensor_scalar(g_root.bitcast(I32), g_half.bitcast(I32), -0.5, RSQRT_SEED, ALU.mult, ALU.add))
            for _ in range(3):
                own.done(dve.tensor_tensor(g_tmp, g_root, g_root, ALU.mult))
                own.done(dve.tensor_tensor(g_tmp, g_tmp, g_half, ALU.mult))
                own.done(dve.tensor_scalar(g_tmp, g_tmp, -1.0, 1.5, ALU.mult, ALU.add))
                own.done(dve.tensor_tensor(g_root, g_root, g_tmp, ALU.mult))
            dve.tensor_scalar(gnorm, guides[:, :], g_root, None, ALU.mult).then_inc(setup_dve, 1)
            dve.wait_ge(setup_pe, 1)
            dve.tensor_copy(silu_t, pair[0][0][:, 0:n_seq]).then_inc(setup_dve, 1)
            dve.wait_ge(setup_pe, 2)
            dve.tensor_copy(dots_by[:, 0:GUIDES], pair[0][1][:, 0:GUIDES])
            dve.tensor_copy(dots_by[:, GUIDES:], eye_s[:, :])
            dve.wait_ge(setup_pe, 3)
            dve.tensor_copy(columns[:, :], pair[1][0][:, 0:N_ROWS])
            dve.wait_ge(setup_pe, 4)
            own.done(dve.tensor_copy(mod[:, :, :], pair[1][1][:, 0:6 * n_seq].rearrange("p (m s) -> p m s", m=6)))
            for row in (MOD_CA, MOD_CB):
                dve.tensor_scalar(mod[:, row, :], mod[:, row, :], 1.0, None, ALU.add)
            for row in (MOD_GA, MOD_GB):
                gate = mod[:, row, :]
                own.done(dve.tensor_scalar(sign, gate, 0.0, 2.0, ALU.is_ge, ALU.mult))
                own.done(dve.scalar_tensor_tensor(gate, gate, -1.0, gate, ALU.mult, ALU.max))
                own.done(dve.tensor_scalar(gate, gate, 0.25, None, ALU.max))
                own.done(dve.scalar_tensor_tensor(gate, sign, -1.0, gate, ALU.add, ALU.mult))
            dve.tensor_copy(gate_wide, mod[:, MOD_GA, :].rearrange("p (s o) -> p s o", o=1)
                            .broadcast_to([P, n_seq, P])).then_inc(setup_dve, 1)
            dve.wait_ge(setup_pe, 5)
            for k, ps in enumerate((dense[0], dense[1], dense[2], mixed)):
                last = dve.tensor_copy(gate_a[:, 4 * k:4 * k + 4, :].rearrange("p s d -> p (s d)"), ps[:, :])
            last.then_inc(setup_dve, 1)
            dve.wait_ge(w_in, 32)
            dve.tensor_copy(wq_hi[:, :, :], stage_q)
            own.done(dve.tensor_copy(w1_hi[:, :, :], stage_1))
            dve.tensor_tensor(wq_lo[:, :, :], stage_q, wq_hi[:, :, :].bitcast(F32), ALU.subtract).then_inc(weights_ready, 1)
            dve.tensor_tensor(w1_lo[:, :, :], stage_1, w1_hi[:, :, :].bitcast(F32), ALU.subtract).then_inc(weights_ready, 1)

            def attention(i, slot, step):
                s, layer, before = att(i, slot)
                what = step[1]
                if what == "project":
                    dve.wait_ge(projected, before + 1)
                    dve.tensor_tensor(flat(y_t[s]), flat(y_t[s]), mixed[:, :], ALU.add).then_inc(attended, 1)
                    return
                t = step[2]
                tau = before * 4 + t
                if what == "score":
                    for m in range(2):
                        dve.wait_ge(scored, 2 * tau + m + 1)
                        dve.tensor_reduce(neg_max[:, 2 * (t % 2) + m, :],
                                          pair[t % 2][m][:, :].rearrange("p (k n) -> p k n", k=4), AX_X, ALU.max,
                                          negate=True).then_inc(maxed, 1)
                elif what == "mix":
                    for m in range(2):
                        heads = mixed[:, 0:4 * VW].rearrange("p (k n) -> p k n", k=4)
                        dve.wait_ge(mixed_full, 2 * tau + m + 1)
                        dve.reciprocal(sum_p[:, m, :], heads[:, :, DH]).then_inc(mix_self, 1)
                        dve.wait_ge(mix_self, 2 * tau + m + 1)
                        if past(tau - 1):
                            dve.wait_ge(out_turned, tau - 1)
                        dve.tensor_tensor(
                            o_rows[:, t % 2, :].rearrange("p (k m d) -> p k m d", k=4, m=2)[:, :, m, :], heads[:, :, 0:DH],
                            sum_p[:, m, :].rearrange("p (k o) -> p k o", o=1).broadcast_to([P, 4, DH]),
                            ALU.mult).then_inc(mix_normed, 1)

            def layer_stats(src, moments_, mean_var_, half_, root_, chain, seeded):
                for j in range(TILES):
                    last = dve.bn_stats(moments_[:, j, :], src(j))
                chain.done(last, fixed=True)
                for j in range(TILES):
                    last = dve.bn_aggr(mean_var_[:, j, :], moments_[:, j, :])
                chain.done(last)
                chain.done(dve.tensor_scalar(half_, mean_var_[:, :, 1], 1e-5, 0.5, ALU.add, ALU.mult))
                rsqrt_seed(root_, half_, seeded)

            def normalise(to, src, mean_var_, root_):
                for j in range(TILES):
                    last = dve.tensor_scalar(to(j), src(j), mean_var_[:, j, 0:1], root_[:, j:j + 1], ALU.subtract, ALU.mult)
                return last

            def feed_forward(i, slot, step):
                layer, before, _ = ff(i, slot)
                what = step[1]
                if what == "stats":
                    dve.wait_ge(*filled_at(i, slot, step))
                    src = bank(i, slot, step)
                    layer_stats(lambda j: src[:, j * P:(j + 1) * P], moments_f, mean_var_f, half_f[:, :], root_f[:, :],
                                Chain(ff_self, 3 * before), ff_seeded)
                elif what == "norm":
                    dve.wait_ge(ff_rooted, before + 1)
                    src = bank(i, slot, (FF, "stats"))
                    normalise(lambda j: hn[:, j * P:(j + 1) * P], lambda j: src[:, j * P:(j + 1) * P],
                              mean_var_f, root_f).then_inc(empty(i, slot, (FF, "stats")), 1)
                    dve.wait_ge(*read_at(i, slot, step))
                    dve.tensor_copy(h_hi[:, :], hn[:, :]).then_inc(ff_hi, 1)
                elif what == "up":
                    chunk = step[2]
                    n = HID_CHUNKS[chunk][1]
                    dve.wait_ge(*read_at(i, slot, step, 0))
                    dve.wait_ge(*filled_at(i, slot, step, 1))
                    src = bank(i, slot, step, 1)
                    row = ROW_B1 + 6 * layer + chunk
                    dve.scalar_tensor_tensor(hidden[0:n, chunk, :], src[0:n, :], columns[0:n, row:row + 1],
                                             gelu[0:n, chunk % 2, :], ALU.add, ALU.mult).then_inc(empty(i, slot, step, 1), 1)
                elif what == "down":
                    dve.wait_ge(*filled_at(i, slot, step))
                    src = bank(i, slot, step)
                    row = ROW_B2 + layer
                    stream_y = flat(y_t[stream(slot)])
                    dve.scalar_tensor_tensor(stream_y, src[:, :], columns[:, row:row + 1], stream_y, ALU.add,
                                             ALU.add).then_inc(empty(i, slot, step), 1)

            NEW_SELF = 3 + 1 + 6 + 2 + 2 + 3

            def new_unit(i, slot, step):
                before = new(i, slot)
                s = stream(slot)
                what = step[1]
                base = NEW_SELF * before
                if what == "stats":
                    dve.wait_ge(x_loaded[s], 16 * (i + 1))
                    layer_stats(lambda j: x_in[s][:, j, :], moments, mean_var, half_n[:, :], root_n[:, :],
                                Chain(new_self, base), new_seeded)
                elif what == "turn":
                    dve.wait_ge(new_rooted, 3 * before + 1)
                    normalise(lambda j: xn[:, j, :], lambda j: x_in[s][:, j, :], mean_var, root_n).then_inc(new_normed, 1)
                elif what == "dots":
                    own = Chain(new_self, base + 3)
                    dve.wait_ge(new_squares, before + 1)
                    own.done(dve.tensor_scalar(half_n[:, :], col[:, SS, :], 1e-30, 0.5, ALU.max, ALU.mult))
                    rsqrt_seed(root_n[:, :], half_n[:, :], new_seeded)
                    for m in range(2):
                        src = bank(i, slot, step, m)
                        dots = src[:, 0:2 * (GUIDES + P)].rearrange("p (k n) -> p k n", k=2)[:, :, 0:GUIDES]
                        dve.tensor_reduce(col[:, DMAX, 2 * m:2 * m + 2], dots, AX_X, ALU.max)
                elif what == "sims":
                    own = Chain(new_self, base + 4)
                    dve.wait_ge(new_rooted, 3 * before + 2)
                    own.done(dve.tensor_tensor(col[:, MAG, :], col[:, SS, :], root_n[:, :], ALU.mult))
                    own.done(dve.scalar_tensor_tensor(col[:, RM, :], col[:, MAG, :], 1e-6, root_n[:, :], ALU.is_gt, ALU.mult))
                    own.done(dve.tensor_tensor(col[:, AN, :], col[:, MAG, :], col[:, RM, :], ALU.mult))
                    own.done(dve.tensor_scalar(col[:, ANM, :], col[:, AN, :], 1e-8, None, ALU.max))
                    own.done(dve.reciprocal(col[:, RAN, :], col[:, ANM, :]))
                    own.done(dve.scalar_tensor_tensor(col[:, F_SIM, :], col[:, RM, :], 2.0, col[:, RAN, :], ALU.mult, ALU.mult))
                    dve.scalar_tensor_tensor(col[:, BIAS, :], col[:, DMAX, :], -1.0, col[:, F_SIM, :], ALU.mult,
                                             ALU.mult).then_inc(new_sims, 1)
                elif what == "weights":
                    own = Chain(new_self, base + 10)
                    dve.wait_ge(new_exp, before + 1)
                    own.done(dve.reciprocal(col[:, RSUM_E, :], col[:, SUM_E, :]))
                    dve.scalar_tensor_tensor(col[:, CN, :], col[:, TANH, :], 1.0 - GUIDANCE, col[:, RM, :], ALU.mult, ALU.mult)
                    own.done(dve.scalar_tensor_tensor(col[:, CW, :], col[:, TANH, :], GUIDANCE, col[:, RSUM_E, :], ALU.mult,
                                                      ALU.mult))
                    dve.tensor_copy(weighed[:, :, P:P + 1], col[:, TANH, :].rearrange("p (j o) -> p j o", o=1))
                    for m in range(2):
                        src = bank(i, slot, (NEW, "dots"), m)
                        steps = src[:, 0:2 * (GUIDES + P)].rearrange("p (k n) -> p k n", k=2)[:, :, GUIDES:]
                        dve.tensor_tensor(weighed[:, 2 * m:2 * m + 2, 0:P], steps,
                                          col[:, CN, 2 * m:2 * m + 2].rearrange("p (j o) -> p j o", o=1)
                                          .broadcast_to([P, 2, P]), ALU.mult).then_inc(empty(i, slot, (NEW, "dots"), m), 1)
                    dve.tensor_tensor(weighed[:, :, P + 1:], expd, col[:, CW, :].rearrange("p (j o) -> p j o", o=1)
                                      .broadcast_to([P, TILES, GUIDES]), ALU.mult).then_inc(new_weighed, 1)
                elif what == "gate":
                    own = Chain(new_self, base + 12)
                    for m in range(2):
                        dve.wait_ge(*filled_at(i, slot, (NEW, "sum"), m))
                        src = bank(i, slot, (NEW, "sum"), m)
                        last = dve.tensor_scalar(col[:, WS, 2 * m:2 * m + 2],
                                                 src[:, 0:2 * VS].rearrange("p (k n) -> p k n", k=2)[:, :, P],
                                                 1e-8, None, ALU.max)
                    own.done(last)
                    own.done(dve.reciprocal(col[:, RWS, :], col[:, WS, :]))
                    for j in range(TILES):
                        m, k = j // 2, j % 2
                        at = i * 4 + 2 * s + j // 2
                        gate = gate_a[:, at, :] if isinstance(i, int) else \
                            gate_a[:, bass.ds(at, 1), :].rearrange("p o d -> p (o d)")
                        src = bank(i, slot, (NEW, "sum"), m)
                        last = dve.scalar_tensor_tensor(x_mid[s][:, j, :], src[:, k * VS:k * VS + P], col[:, RWS, j:j + 1],
                                                        gate, ALU.mult, ALU.mult)
                        if k:
                            last.then_inc(empty(i, slot, (NEW, "sum"), m), 1)
                    dve.wait_ge(*read_at(i, slot, (NEW, "sum"), 1))
                    dve.tensor_tensor(x_mid[s][:, :, :], x_mid[s][:, :, :], x_in[s][:, :, :], ALU.add).then_inc(x_used[s], 1)
                    dve.wait_ge(x_used[s], i + 1)
                    layer_stats(lambda j: x_mid[s][:, j, :], moments, mean_var, half_n[:, :], root_n[:, :],
                                Chain(new_self, base + 14), new_seeded)
                elif what == "stream":
                    dve.wait_ge(new_rooted, 3 * before + 3)
                    normalise(lambda j: xn[:, j, :], lambda j: x_mid[s][:, j, :], mean_var, root_n).then_inc(new_normed, 1)

            def projections(i, slot, step):
                layer, before = proj(i, slot)
                s = stream(slot)
                what = step[1]
                if what == "split":
                    dve.wait_ge(qkv_shifted, before + 1)
                    dve.tensor_copy(h_hi[:, :], flat(shifted)).then_inc(qkv_hi, 1)
                elif what == "tile":
                    t = step[2]
                    tau = 4 * before + t
                    for m in range(2):
                        src = bank(i, slot, step, m)
                        halves = src[:, :].rearrange("p (h a b) -> p h a b", h=HEADS, a=2)
                        if past(2 * tau + m - 3):
                            dve.wait_ge(added, 2 * tau + m - 3)
                        dve.wait_ge(squared, 2 * tau + m + 1)
                        dve.tensor_tensor(turned_c[:, t % 2, m, :].rearrange("p (h a b) -> p h a b", h=HEADS, a=2),
                                          halves, rot(layer, t, 2 * m), ALU.mult)
                        dve.tensor_tensor(turned_s[:, t % 2, m, :].rearrange("p (h a b) -> p h a b", h=HEADS, a=2),
                                          halves[:, :, ::-1, :], rot(layer, t, 2 * m + 1),
                                          ALU.mult).then_inc(empty(i, slot, step, m), 1)
                        dve.tensor_reduce(q_norm[:, 16 * (t % 2) + 8 * m:16 * (t % 2) + 8 * m + 8],
                                          squares[:, m, :].rearrange("p (h d) -> p h d", h=HEADS), AX_X,
                                          ALU.add).then_inc(summed, 1)
                elif what == "rsqrt":
                    pair_ = 2 * before + step[2]
                    dve.wait_ge(summed, 4 * pair_ + 4)
                    dve.tensor_scalar(half[:, :], q_norm[:, :], 1e-24, 0.5, ALU.max, ALU.mult).then_inc(qk_self, 1)
                    dve.wait_ge(qk_self, pair_ + 1)
                    rsqrt_seed(root[:, :], half[:, :], qk_seeded)
                elif what == "unit":
                    pair_ = 2 * before + step[2]
                    dve.wait_ge(qk_rooted, pair_ + 1)
                    dve.wait_ge(added, 4 * pair_ + 4)
                    rows = qk[s][:, 2 * step[2]:2 * step[2] + 2, :].rearrange("p t (h d) -> p (t h) d", d=DH)
                    dve.tensor_tensor(rows, rows, root[:, :].rearrange("p (h o) -> p h o", o=1)
                                      .broadcast_to([P, 4 * HEADS, DH]), ALU.mult).then_inc(qk_ready, 1)

            def take(i, slot, step):
                if step[0] == "a":
                    attention(i, slot, step)
                elif step[0] == FF:
                    feed_forward(i, slot, step)
                elif step[0] == NEW:
                    new_unit(i, slot, step)
                elif step[0] == PROJ:
                    projections(i, slot, step)
                elif step == (STORE, "turn"):
                    dve.wait_ge(*filled_at(i, slot, step))
                    src = bank(i, slot, step)
                    dve.wait_ge(stored, 16 * (new(i, slot) - 1))
                    dve.tensor_tensor(flat(result), src[:, :], flat(x_mid[stream(slot)]), ALU.add).then_inc(
                        empty(i, slot, step), 1)

            every_turn(dve, take)

        @block.gpsimd
        def _(pool):
            for s in range(2):
                pool.memset(v[s][:, :, :, DH:VW], 1.0)
                pool.memset(v_cross[s][:, :, :, DH:VW], 1.0)
            pool.memset(shifted[:, :, 0:1], 0.0)
            pool.memset(step_t[:, :, SEQ - 1:SEQ], 0.0)
            pool.wait_ge(table_in, 64)
            pool.tensor_copy(mask_h[:, :, :, :], masks_s.rearrange("p t (o n) -> p t o n", o=1).broadcast_to([P, 2, 4, P]))
            for l in range(DEPTH):
                for m in range(2):
                    scale = scales_s[:, l, m, :].rearrange("p (o a b) -> p o a b", o=1, a=2)
                    for half_turn in range(2):
                        which = 2 * m + half_turn
                        by = scale[:, :, ::-1, :] if half_turn else scale
                        pool.tensor_tensor(tables[:, l, :, which, :].rearrange("p t (a b) -> p t a b", a=2),
                                           rotary_s[:, :, which, :].rearrange("p t (a b) -> p t a b", a=2),
                                           by.broadcast_to([P, 2, 2, DH // 2]), ALU.mult)
            pool.wait_ge(const_in, 64)
            pool.tensor_copy(eye_h[:, :], eye_s[:, :]).then_inc(setup_pool, 1)

            def newton(root_, half_, scratch_, threes, base_sem, base, done_sem):
                count = base
                for k in range(3):
                    for n, (to, a, b, op) in enumerate(((scratch_, root_, root_, ALU.mult), (scratch_, scratch_, half_, ALU.mult),
                                                        (scratch_, threes, scratch_, ALU.subtract),
                                                        (root_, root_, scratch_, ALU.mult))):
                        ins = pool.tensor_tensor(to, a, b, op)
                        if (k, n) == (2, 3):
                            ins.then_inc(done_sem, 1)
                        else:
                            ins.then_inc(base_sem, 1)
                            count = count + 1
                            pool.wait_ge(base_sem, count)

            def take(i, slot, step):
                s = stream(slot)
                if step == (FF, "stats"):
                    before = ff(i, slot)[1]
                    pool.wait_ge(ff_seeded, before + 1)
                    newton(root_f[:, :], half_f[:, :], scratch_f[:, :], three_halves[:, 0:4], ff_newton, NEWTON * before,
                           ff_rooted)
                elif step == (FF, "norm"):
                    before = ff(i, slot)[1]
                    pool.wait_ge(ff_hi, before + 1)
                    pool.tensor_tensor(h_lo[:, :], hn[:, :], h_hi[:, :].bitcast(F32), ALU.subtract).then_inc(ff_lo, 1)
                elif step in ((NEW, "stats"), (NEW, "dots"), (NEW, "gate")):
                    roots = 3 * new(i, slot) + ("stats", "dots", "gate").index(step[1])
                    pool.wait_ge(new_seeded, roots + 1)
                    newton(root_n[:, :], half_n[:, :], scratch_n[:, :], three_halves[:, 0:4], new_newton, NEWTON * roots,
                           new_rooted)
                elif step == (NEW, "steps"):
                    pool.wait_ge(*read_at(i, slot, (NEW, "turn")))
                    pool.tensor_tensor(step_t[:, :, 0:SEQ - 1], h_a[:, :, 1:SEQ], h_a[:, :, 0:SEQ - 1],
                                       ALU.subtract).then_inc(new_steps, 1)
                elif step[0] == PROJ:
                    before = proj(i, slot)[1]
                    if step[1] == "split":
                        pool.wait_ge(qkv_hi, before + 1)
                        pool.tensor_tensor(h_lo[:, :], flat(shifted), h_hi[:, :].bitcast(F32), ALU.subtract).then_inc(qkv_lo, 1)
                    elif step[1] == "tile":
                        t = step[2]
                        for m in range(2):
                            pool.wait_ge(summed, 2 * (4 * before + t) + m + 1)
                            pool.tensor_tensor(qk[s][:, t, m * INNER:(m + 1) * INNER], turned_c[:, t % 2, m, :],
                                               turned_s[:, t % 2, m, :], ALU.add).then_inc(added, 1)
                    elif step[1] == "rsqrt":
                        pair_ = 2 * before + step[2]
                        pool.wait_ge(qk_seeded, pair_ + 1)
                        newton(root[:, :], half[:, :], scratch[:, :], three_halves[:, :], qk_newton, NEWTON * pair_, qk_rooted)

            every_turn(pool, take)


def shape_constants(np):
    eye = np.eye(P, dtype=np.float32)
    masks = np.full((P, 2, P), -1e30, np.float32)
    i, j = np.arange(WIN)[:, None], np.arange(WIN)[None, :]
    own, before = j <= i, j >= i
    masks[:WIN, 0, :WIN][own] = 0
    masks[:WIN, 1, :WIN][own] = 0
    masks[:WIN, 1, WIN:][before] = 0
    for t in range(2):
        masks[WIN:, t, :WIN][before] = 0
        masks[WIN:, t, WIN:][own] = 0
    reach = 8
    band = np.zeros((SEQ, SEQ), np.float32)
    for pos in range(1, SEQ):
        w = min(pos, reach)
        for k in range(reach - w, reach):
            band[pos - reach + k, pos] = 0.1 + 0.9 * (k - (reach - w)) / (w - 1) if w > 1 else 0.1
    band = band.reshape(2, P, SEQ).transpose(1, 0, 2)
    half = np.arange(0, DH, 2, dtype=np.float32)
    pos = np.arange(SEQ, dtype=np.float32)
    freqs = pos[:, None] * (np.float32(1) / np.float32(10000.0) ** (half / np.float32(DH)))[None, :]
    base = (half + 0.4 * DH) / (1.4 * DH)
    xpos = base[None, :] ** ((pos - SEQ // 2) / (WIN // 2))[:, None]
    cos, sin = np.cos(freqs), np.sin(freqs)
    rotary = np.stack([np.concatenate(pair_, 1) for pair_ in (
        (8 * cos * xpos, 8 * cos * xpos), (-8 * sin * xpos, 8 * sin * xpos),
        (cos / xpos, cos / xpos), (-sin / xpos, sin / xpos))], 1)
    rotary = rotary.reshape(2, P, 4, DH).transpose(1, 0, 2, 3)
    return {"eye": eye, "masks": masks, "band": band, "rotary": rotary.astype(np.float32)}


_INS = ["L0_attn_embeddings", "L0_attn_guidance_trajectories", "L0_ffn_wqkv", "L0_ffn_q_scale", "L0_ffn_k_scale",
        "L0_ffn_wo", "L0_ffn_ln_g", "L0_ffn_ln_b", "L0_ffn_w1", "L0_ffn_b1", "L0_ffn_w2", "L0_ffn_b2", "L0_c", "L0_wmod"]


def kernel(**inputs):
    import numpy as _np
    import concourse.bacc as _bacc
    from concourse import mybir as _mybir
    from concourse.bass_utils import run_bass_kernel_spmd as _run

    nc = _bacc.Bacc("TRN2", target_bir_lowering=False, num_devices=1)
    arrays = {f"in_{name}_dram": _np.ascontiguousarray(inputs[name]) for name in _INS}
    arrays.update({f"const_{name}_dram": _np.ascontiguousarray(a) for name, a in shape_constants(_np).items()})
    args = [nc.dram_tensor(name, a.shape, _mybir.dt.from_np(a.dtype), kind="ExternalInput").ap()
            for name, a in arrays.items()]
    shape = inputs["L0_attn_embeddings"].shape
    args.append(nc.dram_tensor("out_0_dram", shape, _mybir.dt.float32, kind="ExternalOutput").ap())
    adaln_block(nc, *args)
    r = _run(nc, [arrays], core_ids=[0])
    return r.results[0]["out_0_dram"]
```

```python
from contextlib import ExitStack

import concourse.bass as bass
from concourse import mybir

F32 = mybir.dt.float32
F32R = mybir.dt.float32r
BF16 = mybir.dt.bfloat16
I32 = mybir.dt.int32
ALU = mybir.AluOpType
ACT = mybir.ActivationFunctionType
AX_X = mybir.AxisListType.X

P = 128
SEQ = 256
TILES = 4
UNIT = TILES * P
HEADS, DH, WIN = 8, 64, 64
INNER = HEADS * DH
HID = int(P * 4 * 2 / 3)
HID_CHUNKS = [(0, 128), (128, 128), (256, HID - 256)]
GUIDES = 64
DEPTH = 2
QKV = 3 * INNER
GUIDANCE = 0.4
VW = DH + 1
WEIGHED = P + 1 + GUIDES
VS = P + 2
RSQRT_SEED = float(0x5F3759DF - (1 << 22))
NEWTON = 11

ROW_LN_G, ROW_LN_B, ROW_B2, ROW_B1 = 0, DEPTH, 2 * DEPTH, 3 * DEPTH
N_ROWS = ROW_B1 + 6 * DEPTH
MOD_SA, MOD_CA, MOD_GA, MOD_SB, MOD_CB, MOD_GB = range(6)

FF, NEW, PROJ, STORE = "ff", "new", "proj", "store"

def steps(text):
    return [tuple(int(word) if word.isdigit() else word for word in name.split(".")) for name in text.split()]


ORDER = {
    "pe": [*2 * [steps("""
        a.turn.0 a.turn.1 ff.stats a.score.0 a.score.1 a.flip.0 a.mix.0 ff.norm a.out.0 a.flip.1 ff.up.0
        ff.up.1 ff.up.2 ff.down a.mix.1 a.turn.2 a.out.1 a.turn.3 proj.tile.0.0 a.score.2 proj.tile.0.1
        proj.tile.0.2 proj.tile.1.0 a.score.3 proj.tile.1.1 a.flip.2 proj.tile.1.2 proj.tile.2.0 a.mix.2
        proj.tile.2.1 proj.tile.2.2 a.flip.3 proj.tile.3.0 a.mix.3 proj.tile.3.1 a.out.2 a.out.3
        proj.tile.3.2 a.project""")],
        *2 * [steps("""
        a.turn.0 a.turn.1 a.score.0 proj.tile.0.0 proj.tile.0.1 proj.tile.0.2 a.score.1 proj.tile.1.0
        proj.tile.1.1 new.turn proj.tile.1.2 a.flip.0 proj.tile.2.0 proj.tile.2.1 a.mix.0 new.dots a.flip.1
        a.mix.1 a.out.0 ff.stats a.out.1 a.turn.2 a.turn.3 a.score.2 a.score.3 a.flip.2 new.mix
        proj.tile.2.2 a.mix.2 proj.tile.3.0 a.flip.3 ff.norm proj.tile.3.1 a.mix.3 a.out.2 new.sum a.out.3
        proj.tile.3.2 a.project ff.up.0 ff.up.1 ff.up.2 ff.down new.stream store.turn""")]],
    "act": [*2 * [steps("""
        ff.stats a.turn.0 a.turn.1 a.score.0 a.flip.0 a.score.1 ff.norm a.flip.1 ff.up.0 a.out.0 ff.up.1
        ff.up.2 proj.split a.out.1 a.turn.2 proj.tile.0.0 a.turn.3 proj.tile.0.1 proj.tile.0.2 proj.tile.1.0
        a.score.2 proj.tile.1.1 a.flip.2 proj.tile.1.2 proj.tile.2.0 a.score.3 proj.tile.2.1 a.flip.3
        proj.tile.3.0 proj.tile.2.2 a.out.2 a.out.3 proj.tile.3.1 proj.tile.3.2""")],
        *2 * [steps("""
        proj.split a.turn.0 a.turn.1 proj.tile.0.0 proj.tile.0.1 a.score.0 proj.tile.0.2 proj.tile.1.0
        proj.tile.1.1 new.turn proj.tile.1.2 a.flip.0 proj.tile.2.0 proj.tile.2.1 a.score.1 new.dots
        a.flip.1 ff.stats a.out.0 a.out.1 a.turn.2 a.turn.3 new.sims a.score.2 a.flip.2 a.score.3 new.mix
        proj.tile.2.2 proj.tile.3.0 a.flip.3 proj.tile.3.1 ff.norm a.out.2 a.out.3 proj.tile.3.2 ff.up.0
        ff.up.1 ff.up.2 store.scale new.stream""")]],
    "dve": [*2 * [steps("""
        ff.stats a.score.0 a.score.1 ff.norm a.mix.0 ff.hi a.unit ff.up.0 ff.up.1 ff.up.2 ff.down a.mix.1
        proj.split proj.tile.0.0 a.score.2 proj.tile.0.1 proj.tile.1.0 a.score.3 proj.tile.1.1 proj.rsqrt.0
        proj.tile.2.0 a.mix.2 proj.tile.2.1 a.mix.3 proj.tile.3.0 proj.unit.0 proj.tile.3.1 a.project
        proj.rsqrt.1""")],
        *2 * [steps("""
        proj.split new.stats a.score.0 proj.tile.0.0 proj.tile.0.1 new.turn a.score.1 proj.tile.1.0
        proj.tile.1.1 a.unit proj.rsqrt.0 proj.tile.2.0 a.mix.0 proj.tile.2.1 new.dots a.mix.1 ff.stats
        new.sims a.score.2 new.weights a.score.3 ff.norm proj.unit.0 a.mix.2 proj.tile.3.0 a.mix.3
        proj.tile.3.1 ff.hi new.gate new.again ff.up.0 a.project ff.up.1 proj.rsqrt.1 ff.up.2 new.stream
        ff.down store.turn proj.keep""")]],
    "pool": [*2 * [steps("""
        ff.stats a.rsqrt ff.hi proj.split proj.tile.0.0 proj.tile.0.1 proj.tile.1.0 proj.tile.1.1
        proj.rsqrt.0 proj.tile.2.0 proj.tile.2.1 proj.tile.3.0 proj.tile.3.1""")],
        *2 * [steps("""
        proj.split new.stats a.rsqrt proj.tile.0.0 proj.tile.0.1 new.steps proj.tile.1.0 proj.tile.1.1
        new.dots ff.stats proj.rsqrt.0 proj.tile.2.0 proj.tile.2.1 proj.tile.3.0 proj.tile.3.1 ff.hi
        new.again""")]],
}


BANKS_OF = {(FF, "stats"): 1, (FF, "norm"): 1, (FF, "up"): 2, (FF, "down"): 1, (STORE, "turn"): 1,
            (NEW, "turn"): 1, (NEW, "dots"): 2, (NEW, "mix"): 1, (NEW, "sum"): 2, (NEW, "stream"): 1,
            (PROJ, "tile"): 1}
DENSE_BANKS = 3
COS_ON_POOL = (0,)


def unit_of(i, slot, kind):
    if kind == NEW:
        return i if slot == 2 else i + 1
    if kind == PROJ:
        return i - 1 if slot < 2 else i
    if kind == "a":
        return i if slot == 3 else i - 1
    return i - 1


def runs(i, slot, step, turns):
    return not isinstance(i, int) or 0 <= unit_of(i, slot, step[0]) < turns


class BankTurns:

    def __init__(self, turns):
        self.turns = turns
        self.bank = {}
        place = 0
        self.steps = []
        for slot in range(4):
            for step in ORDER["pe"][slot]:
                for n in range(BANKS_OF.get(step[:2], 0) if step[0] != "a" else 0):
                    self.bank[(slot, step, n)] = place % DENSE_BANKS
                    self.steps.append((slot, step, n))
                    place += 1

    def before(self, i, key):
        count = 0
        for other in self.steps:
            if other == key:
                break
            if self.bank[other] == self.bank[key] and runs(i, other[0], other[1], self.turns):
                count += 1
        return count

    def whole(self, i, bank):
        return sum(self.bank[k] == bank and runs(i, k[0], k[1], self.turns) for k in self.steps)

    def of(self, i, slot, step, n=0):
        key = (slot, step, n)
        bank = self.bank[key]
        full = self.whole(None, bank)
        if isinstance(i, int):
            return bank, sum(self.whole(j, bank) for j in range(-1, i)) + self.before(i, key)
        return bank, i * full + (self.whole(-1, bank) + self.whole(0, bank) - full + self.before(None, key))


def past(count):
    return not isinstance(count, int) or count > 0


def adaln_block(nc, x, traj, wqkv, q_scale, k_scale, wo, ln_g, ln_b, w1, b1, w2, b2, c, wmod,
                eye, masks, band, rotary, out):
    n_seq = x.shape[0]
    units = n_seq * SEQ // UNIT
    turns = units // 2
    bank_turns = BankTurns(turns)

    with ExitStack() as ctx:
        def sb(name, shape, dt=F32):
            return ctx.enter_context(nc.sbuf_tensor(name, shape, dt))

        def sem(name):
            return ctx.enter_context(nc.semaphore(name))

        dense = [ctx.enter_context(nc.psum_tensor(f"dense{k}", [P, 512], F32)) for k in range(DENSE_BANKS)]
        pair = [[ctx.enter_context(nc.psum_tensor(f"pair{k}{m}", [P, 512], F32)) for m in range(2)] for k in range(2)]
        mixed = ctx.enter_context(nc.psum_tensor("mixed", [P, 512], F32))

        eye_s = sb("eye_s", [P, P])
        eye_h = sb("eye_h", [P, P], BF16)
        mask_h = sb("mask_h", [P, 2, 4, P], BF16)
        band_s = sb("band_s", [P, 2, SEQ])
        tables = sb("tables", [P, DEPTH, 2, 4, DH])
        three_halves = sb("three_halves", [P, 32])
        columns = sb("columns", [P, N_ROWS])
        guides = sb("guides", [GUIDES, P])
        dots_by = sb("dots_by", [P, GUIDES + P])
        mod = sb("mod", [P, 6, n_seq])
        gate_a = sb("gate_a", [P, n_seq, P])
        wq_hi, wq_lo = sb("wq_hi", [P, DEPTH, QKV], F32R), sb("wq_lo", [P, DEPTH, QKV], F32R)
        w1_hi, w1_lo = sb("w1_hi", [P, DEPTH, 2 * HID], F32R), sb("w1_lo", [P, DEPTH, 2 * HID], F32R)
        wo_s = sb("wo_s", [P, DEPTH, 4, P])
        w2_s = sb("w2_s", [P, DEPTH, 3, P])

        x_in = [sb(f"x_in{s}", [P, TILES, P]) for s in range(2)]
        x_mid = [sb(f"x_mid{s}", [P, TILES, P]) for s in range(2)]
        y_new = [sb(f"y_new{s}", [P, 2, SEQ]) for s in range(2)]
        y_t = [sb(f"y_t{s}", [P, 2, SEQ]) for s in range(2)]
        qk = [sb(f"qk{s}", [P, TILES, 2 * INNER]) for s in range(2)]
        v = [sb(f"v{s}", [P, TILES, HEADS, VW]) for s in range(2)]
        v_cross = [sb(f"v_cross{s}", [P, 2, HEADS, VW]) for s in range(2)]

        xn = sb("xn", [P, TILES, P])
        h_a = sb("h_a", [P, 2, SEQ])
        step_t = sb("step_t", [P, 2, SEQ])
        weighed = sb("weighed", [P, TILES, WEIGHED])
        guide_mix = h_a[0:GUIDES, :, :].rearrange("p a b -> p (a b)")
        expd = xn[:, 0:2, :].rearrange("p t (k n) -> p (t k) n", k=2)
        shifted = sb("shifted", [P, 2, SEQ])
        hn = sb("hn", [P, UNIT])
        result = hn[:, :].rearrange("p (t d) -> p t d", t=TILES)
        h_hi, h_lo = sb("h_hi", [P, UNIT], F32R), sb("h_lo", [P, UNIT], F32R)
        squares = sb("squares", [P, 2, UNIT])
        space = sb("space", [P, 8 * UNIT])
        turned_c = space[:, 0:4 * UNIT].rearrange("p (t m n) -> p t m n", t=2, m=2)
        turned_s = space[:, 4 * UNIT:].rearrange("p (t m n) -> p t m n", t=2, m=2)
        gelu = space[:, 0:2 * UNIT].rearrange("p (c n) -> p c n", c=2)
        hidden = space[:, 2 * UNIT:5 * UNIT].rearrange("p (c n) -> p c n", c=3)

        q_t = sb("q_t", [P, 2, 4, P])
        k_t = sb("k_t", [P, 4, 2 * P])
        probs = sb("probs", [P, 4, 4, P])
        probs_t = sb("probs_t", [P, 4, 4, P])
        o_rows = sb("o_rows", [P, 2, INNER])
        o_t = sb("o_t", [P, 4, UNIT])

        moments = sb("moments", [P, TILES, 6])
        mean_var = sb("mean_var", [P, TILES, 2])
        half, root, scratch = sb("half", [P, 32]), sb("root", [P, 32]), sb("scratch", [P, 32])
        half_f, root_f, scratch_f = sb("half_f", [P, 4]), sb("root_f", [P, 4]), sb("scratch_f", [P, 4])
        moments_f = sb("moments_f", [P, TILES, 6])
        mean_var_f = sb("mean_var_f", [P, TILES, 2])
        half_n, root_n, scratch_n = sb("half_n", [P, 4]), sb("root_n", [P, 4]), sb("scratch_n", [P, 4])
        q_norm = sb("q_norm", [P, 32])
        col = sb("col", [P, 16, 4])
        (SS, MAG, RM, AN, ANM, RAN, F_SIM, BIAS, DMAX, TANH, SUM_E, RSUM_E, CW, CN, WS, RWS) = range(16)
        spare, spare_a = sb("spare", [P, 1]), sb("spare_a", [P, 2])
        neg_max = sb("neg_max", [P, 4, 4])
        sum_p = sb("sum_p", [P, 2, 4])

        stage_q = qk[0][:, :, :].rearrange("p t n -> p (t n)")[:, 0:DEPTH * QKV].rearrange("p (l n) -> p l n", l=DEPTH)
        stage_1 = qk[1][:, :, :].rearrange("p t n -> p (t n)")[:, 0:DEPTH * 2 * HID].rearrange("p (l n) -> p l n", l=DEPTH)
        wmod_s = o_t[:, :, :].rearrange("p k n -> p (k n)")[:, 0:6 * P]
        gate_wide = probs_t[:, :, :, :].rearrange("p a k n -> p (a k) n")[:, 0:n_seq, :]
        places = probs[:, :, :, :].rearrange("p a k n -> p (a k n)")
        rotary_s = places[:, 0:8 * DH].rearrange("p (t w d) -> p t w d", t=2, w=4)
        scales_s = places[:, 8 * DH:12 * DH].rearrange("p (l m d) -> p l m d", l=DEPTH, m=2)
        masks_s = places[:, 12 * DH:12 * DH + 2 * P].rearrange("p (t n) -> p t n", t=2)
        vectors = places[0:N_ROWS, 1024:1024 + P]
        crow = places[0:n_seq, 1152:1152 + P]
        gnorm = places[0:GUIDES, 1280:1280 + P]
        silu_t = places[:, 1408:1408 + n_seq]
        sign = places[:, 1536:1536 + n_seq]

        const_in, w_in, wo_in, rows_in, table_in = sem("const_in"), sem("w_in"), sem("wo_in"), sem("rows_in"), sem("table_in")
        rows_cleared, setup_self = sem("rows_cleared"), sem("setup_self")
        setup_pe, setup_act, setup_dve, setup_pool = (
            sem("setup_pe"), sem("setup_act"), sem("setup_dve"), sem("setup_pool"))
        weights_ready = sem("weights_ready")
        filled = [sem(f"filled{k}") for k in range(DENSE_BANKS)]
        emptied = [sem(f"emptied{k}") for k in range(DENSE_BANKS)]
        x_loaded, x_used, stored = [sem("x_loaded0"), sem("x_loaded1")], [sem("x_used0"), sem("x_used1")], sem("stored")
        ff_shifted, ff_self, ff_seeded, ff_rooted = sem("ff_shifted"), sem("ff_self"), sem("ff_seeded"), sem("ff_rooted")
        ff_newton, new_newton, qk_newton = sem("ff_newton"), sem("new_newton"), sem("qk_newton")
        ff_hi, ff_lo = sem("ff_hi"), sem("ff_lo")
        new_self, new_seeded, new_rooted, new_normed = sem("new_self"), sem("new_seeded"), sem("new_rooted"), sem("new_normed")
        new_steps, new_squares, new_exp = sem("new_steps"), sem("new_squares"), sem("new_exp")
        new_sims, new_weighed = sem("new_sims"), sem("new_weighed")
        qkv_shifted, qkv_hi, qkv_lo = sem("qkv_shifted"), sem("qkv_hi"), sem("qkv_lo")
        squared, summed, cosine_part, added = sem("squared"), sem("summed"), sem("cosine_part"), sem("added")
        qk_self, qk_seeded, qk_rooted, qk_ready = sem("qk_self"), sem("qk_seeded"), sem("qk_rooted"), sem("qk_ready")
        final_scaled = sem("final_scaled")
        turned, kept, scored, maxed = sem("turned"), sem("kept"), sem("scored"), sem("maxed")
        exped, flipped, flip_kept = sem("exped"), sem("flipped"), sem("flip_kept")
        mixed_full, mix_self, mix_normed = sem("mixed_full"), sem("mix_self"), sem("mix_normed")
        out_turned, out_kept, projected, attended = sem("out_turned"), sem("out_kept"), sem("projected"), sem("attended")

        def att(i, slot):
            return 1 - slot % 2, (0, 1, 1, 0)[slot], i * 4 + slot - 3

        def stream(slot):
            return slot % 2

        def ff(i, slot):
            return (0 if slot < 2 else 1), i * 4 + slot - 4, i * 4 + slot - 3

        def new(i, slot):
            return i * 2 + slot - 1

        def store(i, slot):
            return i * 2 + slot - 4

        def proj(i, slot):
            return (1 if slot < 2 else 0), i * 4 + slot - 2

        def bank(i, slot, step, n=0):
            return dense[bank_turns.of(i, slot, step, n)[0]]

        def filled_at(i, slot, step, n=0):
            b, before = bank_turns.of(i, slot, step, n)
            return filled[b], before + 1

        def read_at(i, slot, step, n=0):
            b, before = bank_turns.of(i, slot, step, n)
            return emptied[b], before + 1

        def read_before(i, slot, step, n=0):
            b, before = bank_turns.of(i, slot, step, n)
            return emptied[b], before

        def refilled(i, slot, step, n=0):
            return past(bank_turns.of(i, slot, step, n)[1])

        def empty(i, slot, step, n=0):
            return emptied[bank_turns.of(i, slot, step, n)[0]]

        def every_turn(eng, name, take, after_first=None):
            def turn(i):
                for slot in range(4):
                    for step in ORDER[name][slot]:
                        if runs(i, slot, step, turns):
                            take(i, slot, step)
            turn(-1)
            turn(0)
            if after_first:
                after_first()
            with eng.Fori(1, turns - 1) as i:
                turn(i)
            turn(turns - 1)
            turn(turns)

        def rot(layer, t, which):
            row = tables[:, layer, t % 2, which, :].rearrange("p (o a b) -> p o a b", o=1, a=2)
            return row.broadcast_to([P, HEADS, 2, DH // 2])

        ROW_LOADS = 3 + 4 * DEPTH

        def flat(tile):
            return tile[:, :, :].rearrange("p a b -> p (a b)")

        def of_seq(row, unit, s, b):
            at = unit * 4 + 2 * s + b
            return mod[:, row, at:at + 1] if isinstance(unit, int) else mod[:, row, bass.ds(at, 1)]

        block = ctx.enter_context(nc.Block())

        @block.sync
        def _(sp):
            def load_x(unit, s):
                at = unit * 4 + 2 * s
                seqs = x[bass.ds(at, 2)] if not isinstance(unit, int) else x[at:at + 2]
                sp.dma_start(x_in[s][:, :, :], seqs.rearrange("b (t p) d -> p (b t) d", p=P)).then_inc(x_loaded[s], 16)

            load_x(0, 0)
            sp.dma_start(eye_s[:, :], eye).then_inc(const_in, 16)
            sp.dma_start(crow, c).then_inc(const_in, 16)
            sp.dma_start(wmod_s, wmod).then_inc(const_in, 16)
            sp.dma_start(guides[:, :], traj).then_inc(const_in, 16)
            sp.dma_start(rotary_s, rotary).then_inc(table_in, 16)
            sp.dma_start(masks_s, masks).then_inc(table_in, 16)
            sp.dma_start(scales_s[:, :, 0, :], q_scale.partition_broadcast(P)).then_inc(table_in, 16)
            sp.dma_start(scales_s[:, :, 1, :], k_scale.partition_broadcast(P)).then_inc(table_in, 16)
            sp.wait_ge(rows_cleared, 1)
            for row, rows in ((ROW_LN_G, ln_g), (ROW_LN_B, ln_b), (ROW_B2, b2)):
                sp.dma_start(vectors[row:row + DEPTH, :], rows).then_inc(rows_in, 16)
            for l in range(DEPTH):
                for m in range(2):
                    row = ROW_B1 + 6 * l + 3 * m
                    sp.dma_start(vectors[row:row + 2, :],
                                 b1[l, m * HID:m * HID + 2 * P].rearrange("(c p) -> c p", p=P)).then_inc(rows_in, 16)
                    sp.dma_start(vectors[row + 2:row + 3, 0:HID - 2 * P],
                                 b1[l:l + 1, m * HID + 2 * P:(m + 1) * HID]).then_inc(rows_in, 16)
            sp.dma_start(stage_q, wqkv.rearrange("l d n -> d l n")).then_inc(w_in, 16)
            sp.dma_start(stage_1, w1.rearrange("l d n -> d l n")).then_inc(w_in, 16)
            sp.dma_start(band_s[:, :, :], band).then_inc(stored, 16)
            load_x(0, 1)
            for l in range(DEPTH):
                sp.dma_start(wo_s[:, l, :, :], wo[l].rearrange("(c p) d -> p c d", p=P)).then_inc(wo_in, 16)
                sp.dma_start(w2_s[:, l, 0:2, :], w2[l, 0:2 * P].rearrange("(c p) d -> p c d", p=P)).then_inc(wo_in, 16)
                sp.dma_start(w2_s[0:HID - 2 * P, l, 2, :], w2[l, 2 * P:HID]).then_inc(wo_in, 16)

            def store_result(i, slot):
                s = stream(slot)
                sp.wait_ge(*read_at(i, slot, (STORE, "turn")))
                at = (i - 1) * 4 + 2 * s
                seqs = out[bass.ds(at, 2)] if not isinstance(i, int) else out[at:at + 2]
                sp.dma_start(seqs.rearrange("b (t p) d -> p (b t) d", p=P), result).then_inc(stored, 16)

            def turn(i, last):
                for slot in (2, 3):
                    s = stream(slot)
                    if runs(i, slot, (STORE, "turn"), turns):
                        store_result(i, slot)
                    if not last:
                        sp.wait_ge(x_used[s], i + 1)
                        load_x(i + 1, s)
            turn(0, False)
            with sp.Fori(1, turns - 1) as i:
                turn(i, False)
            turn(turns - 1, True)
            turn(turns, True)
            sp.wait_ge(stored, 16 * (units + 1))

        @block.tensor
        def _(pe):
            def done(ins, i, slot, step, n=0):
                ins.then_inc(filled[bank_turns.of(i, slot, step, n)[0]], 1)

            def turn_four(to, rows):
                for k in range(4):
                    last = pe.transpose(to[:, k * P:(k + 1) * P], rows(k), eye_s[:, :])
                return last

            pe.wait_ge(const_in, 64)
            pe.wait_ge(setup_act, 1)
            pe.transpose(pair[0][0][:, 0:n_seq], crow, eye_s[0:n_seq, 0:n_seq]).then_inc(setup_pe, 1)
            pe.wait_ge(setup_dve, 1)
            pe.transpose(pair[0][1][:, 0:GUIDES], gnorm, eye_s[0:GUIDES, 0:GUIDES]).then_inc(setup_pe, 1)
            pe.wait_ge(rows_in, 16 * ROW_LOADS)
            pe.transpose(pair[1][0][:, 0:N_ROWS], vectors, eye_s[0:N_ROWS, 0:N_ROWS]).then_inc(setup_pe, 1)
            pe.wait_ge(setup_dve, 2)
            for m in range(6):
                last = pe.matmul(pair[1][1][:, m * n_seq:(m + 1) * n_seq], wmod_s[:, m * P:(m + 1) * P], silu_t,
                                 start=True, stop=True)
            last.then_inc(setup_pe, 1)
            pe.wait_ge(setup_dve, 3)
            for b in range(n_seq):
                to = pair[b // 8][b // 4 % 2]
                last = pe.matmul(to[:, (b % 4) * P:(b % 4 + 1) * P], gate_wide[:, b, :], eye_s[:, :], start=True, stop=True)
            last.then_inc(setup_pe, 1)
            pe.wait_ge(setup_pool, 1)
            pe.wait_ge(stored, 16)

            def attention(i, slot, step):
                s, layer, before = att(i, slot)
                what = step[1]
                if what == "project":
                    pe.wait_ge(out_kept, before * 4 + 4)
                    for k in range(4):
                        last = pe.matmul(mixed[:, :], wo_s[:, layer, k, :], o_t[:, k, :], start=(k == 0), stop=(k == 3))
                    last.then_inc(projected, 1)
                    return
                t = step[2]
                tau = before * 4 + t
                banks = pair[t % 2]
                if what == "turn":
                    pe.wait_ge(qk_ready, 2 * before + t // 2 + 1)
                    if past(tau - 1):
                        pe.wait_ge(out_kept, tau - 1)
                    if past(2 * tau - 2):
                        pe.wait_ge(flip_kept, 2 * tau - 2)
                    turn_four(banks[0], lambda k: qk[s][:, t, k * P:(k + 1) * P]).then_inc(turned, 1)
                    turn_four(banks[1], lambda k: qk[s][:, t, INNER + k * P:INNER + (k + 1) * P]).then_inc(turned, 1)
                elif what == "score":
                    pe.wait_ge(kept, 2 * tau + 2)
                    for m in range(2):
                        pe.matmul(banks[m][:, :], eye_h[:, :], mask_h[:, t % 2, :, :], start=True, stop=False,
                                  skip_group_check=True)
                    for hh in range(4):
                        for w in range(2):
                            for m in range(2):
                                rows = slice(DH * m, DH * (m + 1))
                                keys = k_t[rows, hh, :]
                                if t % 2:
                                    keys = keys[:, 0:P] if w else \
                                        keys.rearrange("p (a b) -> p a b", b=WIN)[:, 0:4:3, :]
                                else:
                                    keys = keys[:, P:2 * P] if w else keys[:, P:P + WIN]
                                n = WIN if (t % 2 == 0 and w == 0) else P
                                last = pe.matmul(banks[m][w * WIN:(w + 1) * WIN, hh * P:hh * P + n],
                                                 q_t[rows, t % 2, hh, w * WIN:(w + 1) * WIN], keys,
                                                 start=False, stop=True, skip_group_check=True)
                                if hh == 3 and w == 1:
                                    last.then_inc(scored, 1)
                elif what == "flip":
                    for m in range(2):
                        pe.wait_ge(exped, 2 * tau + m + 1)
                        turn_four(banks[m], lambda k: probs[:, 2 * (t % 2) + m, k, :]).then_inc(flipped, 1)
                elif what == "mix":
                    for m in range(2):
                        pe.wait_ge(flip_kept, 2 * tau + m + 1)
                        if m == 0 and past(2 * tau):
                            pe.wait_ge(mix_normed, 2 * tau - 1)
                        if t == 0 and m == 0:
                            if past(before):
                                pe.wait_ge(attended, before)
                        if m == 0:
                            if slot:
                                pe.wait_ge(*read_at(i, slot - 1, (PROJ, "tile", t, 2)))
                        for hh in range(4):
                            head = 2 * hh + m
                            for w in range(2):
                                values = v_cross[s][:, t // 2, head, :] if (t % 2 and w == 0) else v[s][:, t, head, :]
                                last = pe.matmul((mixed, banks[1])[m][w * WIN:(w + 1) * WIN, hh * VW:(hh + 1) * VW],
                                                 probs_t[:, 2 * (t % 2) + m, hh, w * WIN:(w + 1) * WIN], values,
                                                 start=True, stop=True)
                        last.then_inc(mixed_full, 1)
                elif what == "out":
                    pe.wait_ge(mix_normed, 2 * tau + 2)
                    turn_four(banks[0], lambda k: o_rows[:, t % 2, k * P:(k + 1) * P]).then_inc(out_turned, 1)

            def split_product(to, w_hi, w_lo, h_cols):
                pe.matmul(to, w_hi, h_hi[:, h_cols], start=True, stop=False)
                pe.matmul(to, w_hi, h_lo[:, h_cols], start=False, stop=False)
                return pe.matmul(to, w_lo, h_hi[:, h_cols], start=False, stop=True)

            def feed_forward(i, slot, step):
                layer, before, _ = ff(i, slot)
                what = step[1]
                if what == "stats":
                    pe.wait_ge(ff_shifted, before + 1)
                    if refilled(i, slot, step):
                        pe.wait_ge(*read_before(i, slot, step))
                    to = bank(i, slot, step)
                    done(turn_four(to, lambda k: flat(shifted)[:, k * P:(k + 1) * P]),
                         i, slot, step)
                elif what == "norm":
                    pe.wait_ge(*read_at(i, slot, (FF, "stats")))
                    if refilled(i, slot, step):
                        pe.wait_ge(*read_before(i, slot, step))
                    to = bank(i, slot, step)
                    done(turn_four(to, lambda k: hn[:, k * P:(k + 1) * P]), i, slot, step)
                elif what == "up":
                    at, n = HID_CHUNKS[step[2]]
                    if step[2] == 0:
                        pe.wait_ge(ff_lo, before + 1)
                    for m, base in enumerate((HID, 0)):
                        if refilled(i, slot, step, m):
                            pe.wait_ge(*read_before(i, slot, step, m))
                        to = bank(i, slot, step, m)
                        cols = slice(base + at, base + at + n)
                        done(split_product(to[0:n, :], w1_hi[:, layer, cols], w1_lo[:, layer, cols], slice(0, UNIT)),
                             i, slot, step, m)
                elif what == "down":
                    if refilled(i, slot, step):
                        pe.wait_ge(*read_before(i, slot, step))
                    to = bank(i, slot, step)
                    for k, (_, n) in enumerate(HID_CHUNKS):
                        pe.wait_ge(*read_at(i, slot, (FF, "up", k), 1))
                        last = pe.matmul(to[:, :], w2_s[0:n, layer, k, :], hidden[0:n, k, :], start=(k == 0), stop=(k == 2))
                    done(last, i, slot, step)

            def new_unit(i, slot, step):
                before = new(i, slot)
                what = step[1]
                if what == "turn":
                    pe.wait_ge(new_normed, 2 * before + 1)
                    if refilled(i, slot, step):
                        pe.wait_ge(*read_before(i, slot, step))
                    to = bank(i, slot, step)
                    done(turn_four(to, lambda k: xn[:, k, :]), i, slot, step)
                elif what == "dots":
                    pe.wait_ge(new_steps, before + 1)
                    for m in range(2):
                        if refilled(i, slot, step, m):
                            pe.wait_ge(*read_before(i, slot, step, m))
                        to = bank(i, slot, step, m)
                        for k in range(2):
                            j = 2 * m + k
                            last = pe.matmul(to[:, k * (GUIDES + P):(k + 1) * (GUIDES + P)],
                                             step_t[:, j // 2, (j % 2) * P:(j % 2 + 1) * P], dots_by[:, :],
                                             start=True, stop=True)
                        done(last, i, slot, step, m)
                elif what == "mix":
                    pe.wait_ge(new_weighed, before + 1)
                    if refilled(i, slot, step):
                        pe.wait_ge(*read_before(i, slot, step))
                    to = bank(i, slot, step)
                    for b in range(2):
                        pe.matmul(to[0:GUIDES, b * SEQ:(b + 1) * SEQ], weighed[:, 2 * b, P + 1:P + 1 + GUIDES],
                                  band_s[:, 0, :], start=True, stop=False, skip_group_check=True)
                        last = pe.matmul(to[0:GUIDES, b * SEQ + P:(b + 1) * SEQ], weighed[:, 2 * b + 1, P + 1:P + 1 + GUIDES],
                                         band_s[:, 1, P:SEQ], start=False, stop=True, skip_group_check=True)
                    done(last, i, slot, step)
                elif what == "sum":
                    pe.wait_ge(*read_at(i, slot, (NEW, "mix")))
                    for m in range(2):
                        if refilled(i, slot, step, m):
                            pe.wait_ge(*read_before(i, slot, step, m))
                        to = bank(i, slot, step, m)
                        for k in range(2):
                            o = to[:, k * VS:k * VS + P + 1]
                            pe.matmul(o, band_s[:, 0, k * P:(k + 1) * P], weighed[:, 2 * m, 0:P + 1], start=True,
                                      stop=False, skip_group_check=True)
                            if k:
                                pe.matmul(o, band_s[:, 1, P:SEQ], weighed[:, 2 * m + 1, 0:P + 1], start=False,
                                          stop=False, skip_group_check=True)
                            j = 2 * m + k
                            last = pe.matmul(to[:, k * VS:k * VS + P], guide_mix[:, j * P:(j + 1) * P], guides[:, :],
                                             start=False, stop=True, skip_group_check=True)
                        done(last, i, slot, step, m)
                elif what == "stream":
                    pe.wait_ge(new_normed, 2 * before + 2)
                    if refilled(i, slot, step):
                        pe.wait_ge(*read_before(i, slot, step))
                    to = bank(i, slot, step)
                    done(turn_four(to, lambda k: xn[:, k, :]), i, slot, step)

            def projections(i, slot, step):
                layer, before = proj(i, slot)
                if step[1] != "tile":
                    return
                t, m = step[2:]
                if t == 0 and m == 0:
                    pe.wait_ge(qkv_lo, before + 1)
                    if isinstance(i, int) and i == 0 and slot == 2:
                        pe.wait_ge(weights_ready, 2)
                        pe.wait_ge(setup_dve, 4)
                        pe.wait_ge(wo_in, 16 * 3 * DEPTH)
                rows = slice(t * P, (t + 1) * P)
                if refilled(i, slot, step):
                    pe.wait_ge(*read_before(i, slot, step))
                to = bank(i, slot, step)
                cols = slice(m * INNER, (m + 1) * INNER)
                pe.matmul(to[:, :], h_hi[:, rows], wq_hi[:, layer, cols], start=True, stop=False)
                pe.matmul(to[:, :], h_hi[:, rows], wq_lo[:, layer, cols], start=False, stop=False)
                done(pe.matmul(to[:, :], h_lo[:, rows], wq_hi[:, layer, cols], start=False, stop=True), i, slot, step)

            def take(i, slot, step):
                if step[0] == "a":
                    attention(i, slot, step)
                elif step[0] == FF:
                    feed_forward(i, slot, step)
                elif step[0] == NEW:
                    new_unit(i, slot, step)
                elif step[0] == PROJ:
                    projections(i, slot, step)
                elif step == (STORE, "turn"):
                    pe.wait_ge(final_scaled, store(i, slot) + 1)
                    if refilled(i, slot, step):
                        pe.wait_ge(*read_before(i, slot, step))
                    to = bank(i, slot, step)
                    done(turn_four(to, lambda k: hn[:, k * P:(k + 1) * P]), i, slot, step)

            def after_first():
                for t in range(TILES):
                    pe.wait_ge(*read_at(0, 3, (PROJ, "tile", t, 2)))

            every_turn(pe, "pe", take, after_first)


        @block.scalar
        def _(act):
            act.wait_ge(const_in, 64)
            act.activation(crow, crow, ACT.Silu).then_inc(setup_act, 1)

            def attention(i, slot, step):
                s, layer, before = att(i, slot)
                if step[1] in ("project", "mix", "unit"):
                    return
                what, t = step[1:]
                tau = before * 4 + t
                banks = pair[t % 2]
                if what == "turn":
                    act.wait_ge(turned, 2 * tau + 1)
                    used = 2 * tau if t % 2 == 0 else 2 * tau - 2
                    if past(used):
                        act.wait_ge(scored, used)
                    act.activation(q_t[:, t % 2, :, :], banks[0][:, :].rearrange("p (k n) -> p k n", k=4),
                                   ACT.Copy).then_inc(kept, 1)
                    act.wait_ge(turned, 2 * tau + 2)
                    cols = slice(0, P) if t % 2 else slice(P, 2 * P)
                    act.activation(k_t[:, :, cols], banks[1][:, :].rearrange("p (k n) -> p k n", k=4),
                                   ACT.Copy).then_inc(kept, 1)
                elif what == "score":
                    for m in range(2):
                        ring = 2 * (t % 2) + m
                        act.wait_ge(maxed, 2 * tau + m + 1)
                        if past(2 * tau + m - 3):
                            act.wait_ge(flipped, 2 * tau + m - 3)
                        for hh in range(4):
                            last = act.activation(probs[:, ring, hh, :], banks[m][:, hh * P:(hh + 1) * P], ACT.Exp,
                                                  bias=neg_max[:, ring, hh:hh + 1], scale=1.0)
                        last.then_inc(exped, 1)
                elif what == "flip":
                    for m in range(2):
                        act.wait_ge(flipped, 2 * tau + m + 1)
                        if past(2 * tau + m - 3):
                            act.wait_ge(mixed_full, 2 * tau + m - 3)
                        act.activation(probs_t[:, 2 * (t % 2) + m, :, :],
                                       banks[m][:, :].rearrange("p (k n) -> p k n", k=4), ACT.Copy).then_inc(flip_kept, 1)
                elif what == "out":
                    act.wait_ge(out_turned, tau + 1)
                    if past(before):
                        act.wait_ge(projected, before)
                    act.activation(o_t[:, :, t * P:(t + 1) * P], banks[0][:, :].rearrange("p (k n) -> p k n", k=4),
                                   ACT.Copy).then_inc(out_kept, 1)

            def shift(src, done_sem):
                act.activation(shifted[0:P // 2, :, :], src[0:P // 2, :, :], ACT.Copy)
                act.activation(shifted[P // 2:P, :, 1:SEQ], src[P // 2:P, :, 0:SEQ - 1], ACT.Copy).then_inc(done_sem, 1)

            def feed_forward(i, slot, step):
                layer, before, att_upto = ff(i, slot)
                what = step[1]
                if what == "stats":
                    act.wait_ge(attended, att_upto)
                    act.wait_ge(qkv_lo, min(proj(i, slot)[1] + slot // 2, 4 * turns) if isinstance(i, int)
                                else proj(i, slot)[1] + slot // 2)
                    shift(y_t[stream(slot)], ff_shifted)
                elif what == "norm":
                    act.wait_ge(*filled_at(i, slot, step))
                    src = bank(i, slot, step)
                    act.activation(hn[:, :], src[:, :], ACT.Identity, scale=columns[:, ROW_LN_G + layer:ROW_LN_G + layer + 1],
                                   bias=columns[:, ROW_LN_B + layer:ROW_LN_B + layer + 1]).then_inc(empty(i, slot, step), 1)
                    act.activation(spare_a[:, 0:1], three_halves[:, 0:1], ACT.Gelu)
                elif what == "up":
                    chunk = step[2]
                    n = HID_CHUNKS[chunk][1]
                    act.wait_ge(*filled_at(i, slot, step, 0))
                    src = bank(i, slot, step, 0)
                    if chunk == 0 and slot > 1 and runs(i, slot, (PROJ, "split"), turns):
                        act.wait_ge(added, 8 * (proj(i, slot)[1] + 1))
                    if chunk == 2:
                        act.wait_ge(*read_at(i, slot, (FF, "up", 0), 1))
                    row = ROW_B1 + 6 * layer + 3 + chunk
                    act.activation(gelu[0:n, chunk % 2, :], src[0:n, :], ACT.Gelu, bias=columns[0:n, row:row + 1],
                                   scale=1.0).then_inc(empty(i, slot, step, 0), 1)
                    if chunk == 2:
                        act.activation(spare_a[:, 1:2], three_halves[:, 0:1], ACT.Exp)

            def new_unit(i, slot, step):
                before = new(i, slot)
                what = step[1]
                if what in ("turn", "stream"):
                    act.wait_ge(*filled_at(i, slot, step))
                    src = bank(i, slot, step)
                    add, scale = (MOD_SA, MOD_CA) if what == "turn" else (MOD_SB, MOD_CB)
                    to = h_a if what == "turn" else y_new[1 - stream(slot)]
                    if what == "stream" and slot == 3 and runs(i, slot, ("a", "project"), turns):
                        act.wait_ge(attended, att(i, slot)[2] + 1)
                    for b in range(2):
                        last = act.activation(to[:, b, :], src[:, b * SEQ:(b + 1) * SEQ], ACT.Identity,
                                              scale=of_seq(scale, unit_of(i, slot, NEW), 1 - stream(slot), b),
                                              bias=of_seq(add, unit_of(i, slot, NEW), 1 - stream(slot), b))
                    last.then_inc(empty(i, slot, step), 1)
                elif what == "dots":
                    for m in range(2):
                        act.wait_ge(*filled_at(i, slot, step, m))
                        src = bank(i, slot, step, m)
                        for k in range(2):
                            j = 2 * m + k
                            at = k * (GUIDES + P) + GUIDES
                            last = act.activation(weighed[:, j, 0:P], src[:, at:at + P], ACT.Square,
                                                  accum_out=col[:, SS, j:j + 1])
                    last.then_inc(new_squares, 1)
                elif what == "sims":
                    act.wait_ge(new_sims, before + 1)
                    act.activation(col[:, TANH, :], col[:, MAG, :], ACT.Tanh, scale=2.0)
                    for j in range(TILES):
                        at = (j % 2) * (GUIDES + P)
                        last = act.activation(expd[:, j, :], bank(i, slot, (NEW, "dots"), j // 2)[:, at:at + GUIDES], ACT.Exp,
                                              scale=col[:, F_SIM, j:j + 1], bias=col[:, BIAS, j:j + 1],
                                              accum_out=col[:, SUM_E, j:j + 1])
                    last.then_inc(new_exp, 1)
                elif what == "mix":
                    act.wait_ge(*filled_at(i, slot, step))
                    src = bank(i, slot, step)
                    act.activation(guide_mix, src[0:GUIDES, :], ACT.Copy).then_inc(empty(i, slot, step), 1)

            def projections(i, slot, step):
                layer, before = proj(i, slot)
                s = stream(slot)
                if step[1] == "split":
                    if slot < 2:
                        act.wait_ge(*read_at(i, slot, (FF, "down")))
                    elif slot == 3:
                        act.wait_ge(*read_at(i, 2, (NEW, "stream")))
                    elif isinstance(i, int) and i == 0:
                        act.wait_ge(*read_at(-1, 3, (NEW, "stream")))
                    shift((y_t if slot < 2 else y_new)[s], qkv_shifted)
                elif step[1] == "tile":
                    t, m = step[2:]
                    tau = 4 * before + t
                    act.wait_ge(*filled_at(i, slot, step))
                    src = bank(i, slot, step)
                    if m < 2:
                        if past(2 * tau + m - 1):
                            act.wait_ge(summed, 2 * tau + m - 1)
                        last = act.activation(squares[:, m, :], src[:, :], ACT.Square)
                        if m in COS_ON_POOL:
                            if past(2 * tau + m - 3):
                                act.wait_ge(added, 2 * tau + m - 3)
                            last = act.activation(turned_c[:, t % 2, m, :], src[:, :], ACT.Copy)
                        last.then_inc(squared, 1)
                    else:
                        half_rows = slice(0, WIN) if t % 2 else slice(WIN, P)
                        heads = src[:, :].rearrange("p (h d) -> p h d", h=HEADS)
                        act.activation(v_cross[s][half_rows, t // 2, :, 0:DH], heads[half_rows], ACT.Copy)
                        act.activation(v[s][:, t, :, 0:DH], heads, ACT.Copy).then_inc(empty(i, slot, step), 1)

            def take(i, slot, step):
                if step[0] == "a":
                    attention(i, slot, step)
                elif step[0] == FF:
                    feed_forward(i, slot, step)
                elif step[0] == NEW:
                    new_unit(i, slot, step)
                elif step[0] == PROJ:
                    projections(i, slot, step)
                elif step == (STORE, "scale"):
                    act.wait_ge(*read_at(i, slot, (FF, "down")))
                    for b in range(2):
                        last = act.activation(hn[:, b * SEQ:(b + 1) * SEQ], y_t[stream(slot)][:, b, :], ACT.Copy,
                                              scale=of_seq(MOD_GB, i - 1, stream(slot), b))
                    last.then_inc(final_scaled, 1)

            every_turn(act, "act", take)

        @block.vector
        def _(dve):
            class Chain:

                def __init__(self, sem_, base):
                    self.sem, self.count = sem_, base

                def done(self, ins, fixed=False):
                    ins.then_inc(self.sem, 1)
                    self.count = self.count + 1
                    dve.wait_ge(self.sem, self.count)
                    if fixed:
                        dve.tensor_copy(spare[:, :], three_halves[:, 0:1])

            def rsqrt_seed(root_, half_, ins_sem):
                dve.tensor_scalar(root_.bitcast(I32), half_.bitcast(I32), -0.5, RSQRT_SEED, ALU.mult, ALU.add).then_inc(ins_sem, 1)

            dve.memset(vectors, 0.0).then_inc(rows_cleared, 1)
            own = Chain(setup_self, 0)
            dve.memset(three_halves[:, :], 1.5)
            dve.wait_ge(const_in, 64)
            g_half, g_root, g_tmp = half[0:GUIDES, 0:1], root[0:GUIDES, 0:1], scratch[0:GUIDES, 0:1]
            own.done(dve.tensor_tensor(gnorm, guides[:, :], guides[:, :], ALU.mult))
            own.done(dve.tensor_reduce(g_half, gnorm, AX_X, ALU.add))
            own.done(dve.tensor_scalar(g_half, g_half, 1e-16, 0.5, ALU.max, ALU.mult))
            own.done(dve.tensor_scalar(g_root.bitcast(I32), g_half.bitcast(I32), -0.5, RSQRT_SEED, ALU.mult, ALU.add))
            for _ in range(3):
                own.done(dve.tensor_tensor(g_tmp, g_root, g_root, ALU.mult))
                own.done(dve.tensor_tensor(g_tmp, g_tmp, g_half, ALU.mult))
                own.done(dve.tensor_scalar(g_tmp, g_tmp, -1.0, 1.5, ALU.mult, ALU.add))
                own.done(dve.tensor_tensor(g_root, g_root, g_tmp, ALU.mult))
            dve.tensor_scalar(gnorm, guides[:, :], g_root, None, ALU.mult).then_inc(setup_dve, 1)
            dve.wait_ge(setup_pe, 1)
            dve.tensor_copy(silu_t, pair[0][0][:, 0:n_seq]).then_inc(setup_dve, 1)
            dve.wait_ge(setup_pe, 2)
            dve.tensor_copy(dots_by[:, 0:GUIDES], pair[0][1][:, 0:GUIDES])
            dve.tensor_copy(dots_by[:, GUIDES:], eye_s[:, :])
            dve.wait_ge(setup_pe, 3)
            dve.tensor_copy(columns[:, :], pair[1][0][:, 0:N_ROWS])
            dve.wait_ge(setup_pe, 4)
            own.done(dve.tensor_copy(mod[:, :, :], pair[1][1][:, 0:6 * n_seq].rearrange("p (m s) -> p m s", m=6)))
            for row in (MOD_CA, MOD_CB):
                dve.tensor_scalar(mod[:, row, :], mod[:, row, :], 1.0, None, ALU.add)
            for row in (MOD_GA, MOD_GB):
                gate = mod[:, row, :]
                own.done(dve.tensor_scalar(sign, gate, 0.0, 2.0, ALU.is_ge, ALU.mult))
                own.done(dve.scalar_tensor_tensor(gate, gate, -1.0, gate, ALU.mult, ALU.max))
                own.done(dve.tensor_scalar(gate, gate, 0.25, None, ALU.max))
                own.done(dve.scalar_tensor_tensor(gate, sign, -1.0, gate, ALU.add, ALU.mult))
            dve.tensor_copy(gate_wide, mod[:, MOD_GA, :].rearrange("p (s o) -> p s o", o=1)
                            .broadcast_to([P, n_seq, P])).then_inc(setup_dve, 1)

            def finish_setup(part):
                if part == 0:
                    dve.wait_ge(setup_pe, 5)
                    for k in range(4):
                        last = dve.tensor_copy(gate_a[:, 4 * k:4 * k + 4, :].rearrange("p s d -> p (s d)"),
                                               pair[k // 2][k % 2][:, :])
                    last.then_inc(setup_dve, 1)
                    dve.wait_ge(w_in, 32)
                    dve.tensor_copy(wq_hi[:, :, :], stage_q)
                    own.done(dve.tensor_copy(w1_hi[:, :, :], stage_1))
                    dve.tensor_tensor(wq_lo[:, :, :], stage_q, wq_hi[:, :, :].bitcast(F32),
                                      ALU.subtract).then_inc(weights_ready, 1)
                else:
                    dve.wait_ge(setup_dve, 4)
                    dve.tensor_tensor(w1_lo[:, :, :], stage_1, w1_hi[:, :, :].bitcast(F32),
                                      ALU.subtract).then_inc(weights_ready, 1)

            def unit_length(s, before, p):
                pair_ = 2 * before + p
                dve.wait_ge(qk_rooted, pair_ + 1)
                dve.wait_ge(added, 4 * pair_ + 4)
                rows = qk[s][:, 2 * p:2 * p + 2, :].rearrange("p t (h d) -> p (t h) d", d=DH)
                dve.tensor_tensor(rows, rows, root[:, :].rearrange("p (h o) -> p h o", o=1)
                                  .broadcast_to([P, 4 * HEADS, DH]), ALU.mult).then_inc(qk_ready, 1)

            def attention(i, slot, step):
                s, layer, before = att(i, slot)
                what = step[1]
                if what == "unit":
                    unit_length(s, before, 1)
                    return
                if what == "project":
                    dve.wait_ge(projected, before + 1)
                    dve.tensor_tensor(flat(y_t[s]), flat((y_t if layer else y_new)[s]), mixed[:, :],
                                      ALU.add).then_inc(attended, 1)
                    return
                t = step[2]
                tau = before * 4 + t
                if what == "score":
                    for m in range(2):
                        dve.wait_ge(scored, 2 * tau + m + 1)
                        dve.tensor_reduce(neg_max[:, 2 * (t % 2) + m, :],
                                          pair[t % 2][m][:, :].rearrange("p (k n) -> p k n", k=4), AX_X, ALU.max,
                                          negate=True).then_inc(maxed, 1)
                elif what == "mix":
                    for m in range(2):
                        heads = (mixed, pair[t % 2][1])[m][:, 0:4 * VW].rearrange("p (k n) -> p k n", k=4)
                        dve.wait_ge(mixed_full, 2 * tau + m + 1)
                        dve.reciprocal(sum_p[:, m, :], heads[:, :, DH]).then_inc(mix_self, 1)
                        dve.wait_ge(mix_self, 2 * tau + m + 1)
                        if past(tau - 1):
                            dve.wait_ge(out_turned, tau - 1)
                        dve.tensor_tensor(
                            o_rows[:, t % 2, :].rearrange("p (k m d) -> p k m d", k=4, m=2)[:, :, m, :], heads[:, :, 0:DH],
                            sum_p[:, m, :].rearrange("p (k o) -> p k o", o=1).broadcast_to([P, 4, DH]),
                            ALU.mult).then_inc(mix_normed, 1)

            def layer_stats(src, moments_, mean_var_, half_, root_, chain, seeded):
                for j in range(TILES):
                    last = dve.bn_stats(moments_[:, j, :], src(j))
                chain.done(last, fixed=True)
                for j in range(TILES):
                    last = dve.bn_aggr(mean_var_[:, j, :], moments_[:, j, :])
                chain.done(last)
                chain.done(dve.tensor_scalar(half_, mean_var_[:, :, 1], 1e-5, 0.5, ALU.add, ALU.mult))
                rsqrt_seed(root_, half_, seeded)

            def normalise(to, src, mean_var_, root_):
                for j in range(TILES):
                    last = dve.tensor_scalar(to(j), src(j), mean_var_[:, j, 0:1], root_[:, j:j + 1], ALU.subtract, ALU.mult)
                return last

            def feed_forward(i, slot, step):
                layer, before, _ = ff(i, slot)
                what = step[1]
                if what == "stats":
                    dve.wait_ge(*filled_at(i, slot, step))
                    src = bank(i, slot, step)
                    layer_stats(lambda j: src[:, j * P:(j + 1) * P], moments_f, mean_var_f, half_f[:, :], root_f[:, :],
                                Chain(ff_self, 3 * before), ff_seeded)
                elif what == "norm":
                    dve.wait_ge(ff_rooted, before + 1)
                    dve.wait_ge(stored, 16 * (max(store(i, slot), store(i, 2)) + 1) if isinstance(i, int)
                                else 16 * (store(i, max(slot, 2)) + 1))
                    src = bank(i, slot, (FF, "stats"))
                    normalise(lambda j: hn[:, j * P:(j + 1) * P], lambda j: src[:, j * P:(j + 1) * P],
                              mean_var_f, root_f).then_inc(empty(i, slot, (FF, "stats")), 1)
                elif what == "hi":
                    if slot > 1 and runs(i, slot, (PROJ, "split"), turns):
                        dve.wait_ge(*filled_at(i, slot, (PROJ, "tile", TILES - 1, 2)))
                    dve.wait_ge(*read_at(i, slot, (FF, "norm")))
                    dve.tensor_copy(h_hi[:, :], hn[:, :]).then_inc(ff_hi, 1)
                elif what == "up":
                    chunk = step[2]
                    n = HID_CHUNKS[chunk][1]
                    dve.wait_ge(*read_at(i, slot, step, 0))
                    dve.wait_ge(*filled_at(i, slot, step, 1))
                    src = bank(i, slot, step, 1)
                    row = ROW_B1 + 6 * layer + chunk
                    dve.scalar_tensor_tensor(hidden[0:n, chunk, :], src[0:n, :], columns[0:n, row:row + 1],
                                             gelu[0:n, chunk % 2, :], ALU.add, ALU.mult).then_inc(empty(i, slot, step, 1), 1)
                elif what == "down":
                    dve.wait_ge(*filled_at(i, slot, step))
                    src = bank(i, slot, step)
                    row = ROW_B2 + layer
                    stream_y = flat(y_t[stream(slot)])
                    dve.scalar_tensor_tensor(stream_y, src[:, :], columns[:, row:row + 1], stream_y, ALU.add,
                                             ALU.add).then_inc(empty(i, slot, step), 1)

            NEW_SELF = 3 + 1 + 6 + 2 + 3 + 3

            def new_unit(i, slot, step):
                before = new(i, slot)
                s = 1 - stream(slot)
                unit = unit_of(i, slot, NEW)
                what = step[1]
                base = NEW_SELF * before
                if what == "stats":
                    dve.wait_ge(x_loaded[s], 16 * (unit + 1))
                    layer_stats(lambda j: x_in[s][:, j, :], moments, mean_var, half_n[:, :], root_n[:, :],
                                Chain(new_self, base), new_seeded)
                elif what == "turn":
                    dve.wait_ge(new_rooted, 3 * before + 1)
                    if slot == 3 and runs(i, 2, step, turns):
                        dve.wait_ge(*filled_at(i, 2, (NEW, "stream")))
                    elif isinstance(i, int) and i == 0:
                        dve.wait_ge(*filled_at(-1, 3, (NEW, "stream")))
                    normalise(lambda j: xn[:, j, :], lambda j: x_in[s][:, j, :], mean_var, root_n).then_inc(new_normed, 1)
                elif what == "dots":
                    own = Chain(new_self, base + 3)
                    dve.wait_ge(new_squares, before + 1)
                    own.done(dve.tensor_scalar(half_n[:, :], col[:, SS, :], 1e-30, 0.5, ALU.max, ALU.mult))
                    rsqrt_seed(root_n[:, :], half_n[:, :], new_seeded)
                    for m in range(2):
                        src = bank(i, slot, step, m)
                        dots = src[:, 0:2 * (GUIDES + P)].rearrange("p (k n) -> p k n", k=2)[:, :, 0:GUIDES]
                        dve.tensor_reduce(col[:, DMAX, 2 * m:2 * m + 2], dots, AX_X, ALU.max)
                elif what == "sims":
                    own = Chain(new_self, base + 4)
                    dve.wait_ge(new_rooted, 3 * before + 2)
                    own.done(dve.tensor_tensor(col[:, MAG, :], col[:, SS, :], root_n[:, :], ALU.mult))
                    own.done(dve.scalar_tensor_tensor(col[:, RM, :], col[:, MAG, :], 1e-6, root_n[:, :], ALU.is_gt, ALU.mult))
                    own.done(dve.tensor_tensor(col[:, AN, :], col[:, MAG, :], col[:, RM, :], ALU.mult))
                    own.done(dve.tensor_scalar(col[:, ANM, :], col[:, AN, :], 1e-8, None, ALU.max))
                    own.done(dve.reciprocal(col[:, RAN, :], col[:, ANM, :]))
                    own.done(dve.scalar_tensor_tensor(col[:, F_SIM, :], col[:, RM, :], 2.0, col[:, RAN, :], ALU.mult, ALU.mult))
                    dve.scalar_tensor_tensor(col[:, BIAS, :], col[:, DMAX, :], -1.0, col[:, F_SIM, :], ALU.mult,
                                             ALU.mult).then_inc(new_sims, 1)
                elif what == "weights":
                    own = Chain(new_self, base + 10)
                    dve.wait_ge(new_exp, before + 1)
                    own.done(dve.reciprocal(col[:, RSUM_E, :], col[:, SUM_E, :]))
                    dve.scalar_tensor_tensor(col[:, CN, :], col[:, TANH, :], 1.0 - GUIDANCE, col[:, RM, :], ALU.mult, ALU.mult)
                    own.done(dve.scalar_tensor_tensor(col[:, CW, :], col[:, TANH, :], GUIDANCE, col[:, RSUM_E, :], ALU.mult,
                                                      ALU.mult))
                    dve.tensor_copy(weighed[:, :, P:P + 1], col[:, TANH, :].rearrange("p (j o) -> p j o", o=1))
                    for m in range(2):
                        src = bank(i, slot, (NEW, "dots"), m)
                        steps = src[:, 0:2 * (GUIDES + P)].rearrange("p (k n) -> p k n", k=2)[:, :, GUIDES:]
                        dve.tensor_tensor(weighed[:, 2 * m:2 * m + 2, 0:P], steps,
                                          col[:, CN, 2 * m:2 * m + 2].rearrange("p (j o) -> p j o", o=1)
                                          .broadcast_to([P, 2, P]), ALU.mult).then_inc(empty(i, slot, (NEW, "dots"), m), 1)
                    dve.tensor_tensor(weighed[:, :, P + 1:], expd, col[:, CW, :].rearrange("p (j o) -> p j o", o=1)
                                      .broadcast_to([P, TILES, GUIDES]), ALU.mult).then_inc(new_weighed, 1)
                elif what == "gate":
                    own = Chain(new_self, base + 12)
                    for m in range(2):
                        dve.wait_ge(*filled_at(i, slot, (NEW, "sum"), m))
                        src = bank(i, slot, (NEW, "sum"), m)
                        last = dve.tensor_scalar(col[:, WS, 2 * m:2 * m + 2],
                                                 src[:, 0:2 * VS].rearrange("p (k n) -> p k n", k=2)[:, :, P],
                                                 1e-8, None, ALU.max)
                    own.done(last)
                    own.done(dve.reciprocal(col[:, RWS, :], col[:, WS, :]))
                    for j in range(TILES):
                        m, k = j // 2, j % 2
                        at = unit * 4 + 2 * s + j // 2
                        gate = gate_a[:, at, :] if isinstance(i, int) else \
                            gate_a[:, bass.ds(at, 1), :].rearrange("p o d -> p (o d)")
                        src = bank(i, slot, (NEW, "sum"), m)
                        last = dve.scalar_tensor_tensor(xn[:, j, :], src[:, k * VS:k * VS + P], col[:, RWS, j:j + 1],
                                                        gate, ALU.mult, ALU.mult)
                        if k:
                            last.then_inc(empty(i, slot, (NEW, "sum"), m), 1)
                    dve.wait_ge(*read_at(i, slot, (NEW, "sum"), 1))
                    own.done(dve.tensor_tensor(flat(x_in[s]), flat(x_in[s]), flat(xn), ALU.add))
                elif what == "again":
                    layer_stats(lambda j: x_in[s][:, j, :], moments, mean_var, half_n[:, :], root_n[:, :],
                                Chain(new_self, base + 15), new_seeded)
                elif what == "stream":
                    dve.wait_ge(new_rooted, 3 * before + 3)
                    normalise(lambda j: xn[:, j, :], lambda j: x_in[s][:, j, :], mean_var, root_n).then_inc(new_normed, 1)

            def projections(i, slot, step):
                layer, before = proj(i, slot)
                s = stream(slot)
                what = step[1]
                if what == "keep":
                    if runs(i, slot, (STORE, "turn"), turns):
                        dve.wait_ge(*read_at(i, slot, (STORE, "turn")))
                    dve.tensor_copy(flat(x_mid[s]), flat(x_in[s])).then_inc(x_used[s], 1)
                elif what == "split":
                    dve.wait_ge(qkv_shifted, before + 1)
                    dve.tensor_copy(h_hi[:, :], flat(shifted)).then_inc(qkv_hi, 1)
                elif what == "tile":
                    t, m = step[2:]
                    if m == 2:
                        return
                    tau = 4 * before + t
                    halves = bank(i, slot, step)[:, :].rearrange("p (h a b) -> p h a b", h=HEADS, a=2)
                    if past(2 * tau + m - 3):
                        dve.wait_ge(added, 2 * tau + m - 3)
                    dve.wait_ge(squared, 2 * tau + m + 1)
                    if m not in COS_ON_POOL:
                        dve.tensor_tensor(turned_c[:, t % 2, m, :].rearrange("p (h a b) -> p h a b", h=HEADS, a=2),
                                          halves, rot(layer, t, 2 * m), ALU.mult)
                    dve.tensor_tensor(turned_s[:, t % 2, m, :].rearrange("p (h a b) -> p h a b", h=HEADS, a=2),
                                      halves[:, :, ::-1, :], rot(layer, t, 2 * m + 1),
                                      ALU.mult).then_inc(empty(i, slot, step), 1)
                    dve.tensor_reduce(q_norm[:, 16 * (t % 2) + 8 * m:16 * (t % 2) + 8 * m + 8],
                                      squares[:, m, :].rearrange("p (h d) -> p h d", h=HEADS), AX_X,
                                      ALU.add).then_inc(summed, 1)
                elif what == "rsqrt":
                    pair_ = 2 * before + step[2]
                    dve.wait_ge(summed, 4 * pair_ + 4)
                    dve.tensor_scalar(half[:, :], q_norm[:, :], 1e-24, 0.5, ALU.max, ALU.mult).then_inc(qk_self, 1)
                    dve.wait_ge(qk_self, pair_ + 1)
                    rsqrt_seed(root[:, :], half[:, :], qk_seeded)
                elif what == "unit":
                    unit_length(s, before, step[2])

            def take(i, slot, step):
                if step[0] == "a":
                    attention(i, slot, step)
                elif step[0] == FF:
                    feed_forward(i, slot, step)
                elif step[0] == NEW:
                    new_unit(i, slot, step)
                    if isinstance(i, int) and i < 0 and step[1] in ("turn", "weights"):
                        finish_setup(("turn", "weights").index(step[1]))
                elif step[0] == PROJ:
                    projections(i, slot, step)
                elif step == (STORE, "turn"):
                    dve.wait_ge(*filled_at(i, slot, step))
                    src = bank(i, slot, step)
                    dve.tensor_tensor(hn[:, :], src[:, :], flat(x_mid[stream(slot)]), ALU.add).then_inc(
                        empty(i, slot, step), 1)

            every_turn(dve, "dve", take)

        @block.gpsimd
        def _(pool):
            for s in range(2):
                pool.memset(v[s][:, :, :, DH:VW], 1.0)
                pool.memset(v_cross[s][:, :, :, DH:VW], 1.0)
            pool.memset(shifted[:, :, 0:1], 0.0)
            pool.memset(step_t[:, :, SEQ - 1:SEQ], 0.0)
            pool.wait_ge(table_in, 64)
            pool.tensor_copy(mask_h[:, :, :, :], masks_s.rearrange("p t (o n) -> p t o n", o=1).broadcast_to([P, 2, 4, P]))
            for l in range(DEPTH):
                for m in range(2):
                    scale = scales_s[:, l, m, :].rearrange("p (o a b) -> p o a b", o=1, a=2)
                    for half_turn in range(2):
                        which = 2 * m + half_turn
                        by = scale[:, :, ::-1, :] if half_turn else scale
                        pool.tensor_tensor(tables[:, l, :, which, :].rearrange("p t (a b) -> p t a b", a=2),
                                           rotary_s[:, :, which, :].rearrange("p t (a b) -> p t a b", a=2),
                                           by.broadcast_to([P, 2, 2, DH // 2]), ALU.mult)
            pool.wait_ge(const_in, 64)
            pool.tensor_copy(eye_h[:, :], eye_s[:, :]).then_inc(setup_pool, 1)

            def newton(root_, half_, scratch_, threes, base_sem, base, done_sem):
                count = base
                for k in range(3):
                    for n, (to, a, b, op) in enumerate(((scratch_, root_, root_, ALU.mult), (scratch_, scratch_, half_, ALU.mult),
                                                        (scratch_, threes, scratch_, ALU.subtract),
                                                        (root_, root_, scratch_, ALU.mult))):
                        ins = pool.tensor_tensor(to, a, b, op)
                        if (k, n) == (2, 3):
                            ins.then_inc(done_sem, 1)
                        else:
                            ins.then_inc(base_sem, 1)
                            count = count + 1
                            pool.wait_ge(base_sem, count)

            def unit_root(pair_):
                pool.wait_ge(qk_seeded, pair_ + 1)
                newton(root[:, :], half[:, :], scratch[:, :], three_halves[:, :], qk_newton, NEWTON * pair_, qk_rooted)

            def take(i, slot, step):
                s = stream(slot)
                if step == (FF, "stats"):
                    before = ff(i, slot)[1]
                    pool.wait_ge(ff_seeded, before + 1)
                    newton(root_f[:, :], half_f[:, :], scratch_f[:, :], three_halves[:, 0:4], ff_newton, NEWTON * before,
                           ff_rooted)
                elif step == (FF, "hi"):
                    before = ff(i, slot)[1]
                    pool.wait_ge(ff_hi, before + 1)
                    pool.tensor_tensor(h_lo[:, :], hn[:, :], h_hi[:, :].bitcast(F32), ALU.subtract).then_inc(ff_lo, 1)
                elif step in ((NEW, "stats"), (NEW, "dots"), (NEW, "again")):
                    roots = 3 * new(i, slot) + ("stats", "dots", "again").index(step[1])
                    pool.wait_ge(new_seeded, roots + 1)
                    newton(root_n[:, :], half_n[:, :], scratch_n[:, :], three_halves[:, 0:4], new_newton, NEWTON * roots,
                           new_rooted)
                elif step == (NEW, "steps"):
                    pool.wait_ge(*read_at(i, slot, (NEW, "turn")))
                    pool.tensor_tensor(step_t[:, :, 0:SEQ - 1], h_a[:, :, 1:SEQ], h_a[:, :, 0:SEQ - 1],
                                       ALU.subtract).then_inc(new_steps, 1)
                elif step[0] == PROJ:
                    layer, before = proj(i, slot)
                    if step[1] == "split":
                        pool.wait_ge(qkv_hi, before + 1)
                        pool.tensor_tensor(h_lo[:, :], flat(shifted), h_hi[:, :].bitcast(F32), ALU.subtract).then_inc(qkv_lo, 1)
                    elif step[1] == "tile":
                        t, m = step[2:]
                        tau = 4 * before + t
                        if m in COS_ON_POOL:
                            pool.wait_ge(squared, 2 * tau + m + 1)
                            raw = turned_c[:, t % 2, m, :].rearrange("p (h a b) -> p h a b", h=HEADS, a=2)
                            pool.tensor_tensor(raw, raw, rot(layer, t, 2 * m), ALU.mult).then_inc(cosine_part, 1)
                            pool.wait_ge(cosine_part, len(COS_ON_POOL) * tau + COS_ON_POOL.index(m) + 1)
                        pool.wait_ge(summed, 2 * tau + m + 1)
                        pool.tensor_tensor(qk[s][:, t, m * INNER:(m + 1) * INNER], turned_c[:, t % 2, m, :],
                                           turned_s[:, t % 2, m, :], ALU.add).then_inc(added, 1)
                    elif step[1] == "rsqrt":
                        unit_root(2 * before + step[2])
                elif step == ("a", "rsqrt"):
                    unit_root(2 * att(i, slot)[2] + 1)

            every_turn(pool, "pool", take)


def shape_constants(np):
    eye = np.eye(P, dtype=np.float32)
    masks = np.full((P, 2, P), -1e30, np.float32)
    i, j = np.arange(WIN)[:, None], np.arange(WIN)[None, :]
    own, before = j <= i, j >= i
    masks[:WIN, 0, :WIN][own] = 0
    masks[:WIN, 1, :WIN][own] = 0
    masks[:WIN, 1, WIN:][before] = 0
    for t in range(2):
        masks[WIN:, t, :WIN][before] = 0
        masks[WIN:, t, WIN:][own] = 0
    reach = 8
    band = np.zeros((SEQ, SEQ), np.float32)
    for pos in range(1, SEQ):
        w = min(pos, reach)
        for k in range(reach - w, reach):
            band[pos - reach + k, pos] = 0.1 + 0.9 * (k - (reach - w)) / (w - 1) if w > 1 else 0.1
    band = band.reshape(2, P, SEQ).transpose(1, 0, 2)
    half = np.arange(0, DH, 2, dtype=np.float32)
    pos = np.arange(SEQ, dtype=np.float32)
    freqs = pos[:, None] * (np.float32(1) / np.float32(10000.0) ** (half / np.float32(DH)))[None, :]
    base = (half + 0.4 * DH) / (1.4 * DH)
    xpos = base[None, :] ** ((pos - SEQ // 2) / (WIN // 2))[:, None]
    cos, sin = np.cos(freqs), np.sin(freqs)
    rotary = np.stack([np.concatenate(pair_, 1) for pair_ in (
        (8 * cos * xpos, 8 * cos * xpos), (-8 * sin * xpos, 8 * sin * xpos),
        (cos / xpos, cos / xpos), (-sin / xpos, sin / xpos))], 1)
    rotary = rotary.reshape(2, P, 4, DH).transpose(1, 0, 2, 3)
    return {"eye": eye, "masks": masks, "band": band, "rotary": rotary.astype(np.float32)}


_INS = ["L0_attn_embeddings", "L0_attn_guidance_trajectories", "L0_ffn_wqkv", "L0_ffn_q_scale", "L0_ffn_k_scale",
        "L0_ffn_wo", "L0_ffn_ln_g", "L0_ffn_ln_b", "L0_ffn_w1", "L0_ffn_b1", "L0_ffn_w2", "L0_ffn_b2", "L0_c", "L0_wmod"]


def kernel(**inputs):
    import numpy as _np
    import concourse.bacc as _bacc
    from concourse import mybir as _mybir
    from concourse.bass_utils import run_bass_kernel_spmd as _run

    nc = _bacc.Bacc("TRN2", target_bir_lowering=False, num_devices=1)
    arrays = {f"in_{name}_dram": _np.ascontiguousarray(inputs[name]) for name in _INS}
    arrays.update({f"const_{name}_dram": _np.ascontiguousarray(a) for name, a in shape_constants(_np).items()})
    args = [nc.dram_tensor(name, a.shape, _mybir.dt.from_np(a.dtype), kind="ExternalInput").ap()
            for name, a in arrays.items()]
    shape = inputs["L0_attn_embeddings"].shape
    args.append(nc.dram_tensor("out_0_dram", shape, _mybir.dt.float32, kind="ExternalOutput").ap())
    adaln_block(nc, *args)
    r = _run(nc, [arrays], core_ids=[0])
    return r.results[0]["out_0_dram"]
```
